# Optimizing a Trainium2 kernel written in Bass

```python
import numpy as np
import jax
import jax.numpy as jnp

def _softmax(x, axis=-1):
    return jax.nn.softmax(x, axis=axis)

def _gelu(x):
    return jax.nn.gelu(x, approximate=True)

def _silu(x):
    return jax.nn.silu(x)

def _sigmoid(x):
    return jax.nn.sigmoid(x)

def _layernorm(x, axis=-1, eps=1e-05):
    m = jnp.mean(x, axis=axis, keepdims=True)
    v = jnp.var(x, axis=axis, keepdims=True)
    return (x - m) / jnp.sqrt(v + eps)

def _scatter_add(tgt, idx, src, axis=0):
    return tgt.at[idx].add(src)

def _segment_sum(src, seg, n):
    return jax.ops.segment_sum(src, seg, n)
kernel_name = 'mk_rec_standalone_d1_rec_r8_c9d8d2'

def setup_inputs(seed: int=0):
    np.random.seed(seed)
    _w = jnp.asarray

    def _rec_inputs():
        import jax
        import jax.numpy as jnp
        _rk = jax.random.key(seed)
        r_x = -0.0002422 + 0.999987 * jax.random.normal(jax.random.fold_in(_rk, 1), (2048, 50, 32), jnp.float32)
        return r_x
    r_x = _rec_inputs()

    def _L0_rec_setup():
        import jax, jax.numpy as jnp
        import numpy as np
        B, N, D, T, HOPS = (2048, 50, 32, 2, 1)
        key = jax.random.key(seed)
        ks = jax.random.split(key, 12)
        s = 0.05
        return {'x': jax.random.normal(ks[0], (B, N, D), jnp.float32), 'masker_param': jax.random.normal(ks[1], (T, N * D, N * N), jnp.float32) * s, 'masker_bias': jax.random.normal(ks[2], (T, N * N), jnp.float32) * s, 'weight': jax.random.normal(ks[3], (HOPS, D, D), jnp.float32) * s, 'w_ih': jax.random.normal(ks[4], (3 * D, D), jnp.float32) * s, 'w_hh': jax.random.normal(ks[5], (3 * D, D), jnp.float32) * s, 'b_ih': jax.random.normal(ks[6], (3 * D,), jnp.float32) * s, 'b_hh': jax.random.normal(ks[7], (3 * D,), jnp.float32) * s, 'bn_gamma': jnp.ones((T * N * D,), jnp.float32), 'bn_beta': jnp.zeros((T * N * D,), jnp.float32), 'ln_gamma': jnp.ones((T, N, D), jnp.float32), 'ln_beta': jnp.zeros((T, N, D), jnp.float32), 'attn_w': jax.random.normal(ks[8], (1, D), jnp.float32) * s, 'attn_b': jax.random.normal(ks[9], (1,), jnp.float32) * s}
    _L0_rec_all = _L0_rec_setup()
    _L0_rec_in = {k: v for k, v in _L0_rec_all.items() if k in ('masker_param', 'masker_bias', 'weight', 'w_ih', 'w_hh', 'b_ih', 'b_hh', 'bn_gamma', 'bn_beta', 'ln_gamma', 'ln_beta', 'attn_w', 'attn_b')}
    del _L0_rec_all
    return {'r_x': r_x, 'L0_rec_masker_param': _L0_rec_in['masker_param'], 'L0_rec_masker_bias': _L0_rec_in['masker_bias'], 'L0_rec_weight': _L0_rec_in['weight'], 'L0_rec_w_ih': _L0_rec_in['w_ih'], 'L0_rec_w_hh': _L0_rec_in['w_hh'], 'L0_rec_b_ih': _L0_rec_in['b_ih'], 'L0_rec_b_hh': _L0_rec_in['b_hh'], 'L0_rec_bn_gamma': _L0_rec_in['bn_gamma'], 'L0_rec_bn_beta': _L0_rec_in['bn_beta'], 'L0_rec_ln_gamma': _L0_rec_in['ln_gamma'], 'L0_rec_ln_beta': _L0_rec_in['ln_beta'], 'L0_rec_attn_w': _L0_rec_in['attn_w'], 'L0_rec_attn_b': _L0_rec_in['attn_b']}

def reference(r_x, L0_rec_masker_param, L0_rec_masker_bias, L0_rec_weight, L0_rec_w_ih, L0_rec_w_hh, L0_rec_b_ih, L0_rec_b_hh, L0_rec_bn_gamma, L0_rec_bn_beta, L0_rec_ln_gamma, L0_rec_ln_beta, L0_rec_attn_w, L0_rec_attn_b):
    import jax
    import jax.numpy as jnp

    def _L0_rec_ref(x, masker_param, masker_bias, weight, w_ih, w_hh, b_ih, b_hh, bn_gamma, bn_beta, ln_gamma, ln_beta, attn_w, attn_b):
        import jax, jax.numpy as jnp
        import numpy as np
        B, N, D, T, HOPS = (2048, 50, 32, 2, 1)
        b, n, d = x.shape
        t = masker_param.shape[0]
        fusion = x.reshape(b, n * d)
        adj = jnp.einsum('bn,tnm->btm', fusion, masker_param) + masker_bias
        adj = jax.nn.relu(adj).reshape(b, t, n, n)
        adj = adj / (adj.sum(axis=-1, keepdims=True) + 1e-06)
        h = jnp.broadcast_to(x[:, None], (b, t, n, d))
        for i in range(weight.shape[0]):
            m = jnp.einsum('btnd,de->btne', h, weight[i])
            m = jnp.einsum('btnm,btmd->btnd', adj, m)
            gates = m @ w_ih.T + b_ih + h @ w_hh.T + b_hh
            r, z, ng = jnp.split(gates, 3, axis=-1)
            r = jax.nn.sigmoid(r)
            z = jax.nn.sigmoid(z)
            ng = jnp.tanh(r * ng)
            h = (1.0 - z) * ng + z * h
        xr = h.reshape(b, t * n * d)
        mu = xr.mean(axis=0)
        var = xr.var(axis=0)
        xr = (xr - mu) / jnp.sqrt(var + 1e-05) * bn_gamma + bn_beta
        h = xr.reshape(b, t, n, d)
        lmu = h.mean(axis=(1, 2, 3), keepdims=True)
        lvar = h.var(axis=(1, 2, 3), keepdims=True)
        h = (h - lmu) / jnp.sqrt(lvar + 1e-05) * ln_gamma + ln_beta
        scores = jnp.squeeze(h @ attn_w.T + attn_b, -1)
        w = jax.nn.softmax(scores, axis=-1)
        out = jnp.einsum('btn,btnd->btd', w, h)
        return out.reshape(b, t * d)
    y = _L0_rec_ref(r_x, L0_rec_masker_param, L0_rec_masker_bias, L0_rec_weight, L0_rec_w_ih, L0_rec_w_hh, L0_rec_b_ih, L0_rec_b_hh, L0_rec_bn_gamma, L0_rec_bn_beta, L0_rec_ln_gamma, L0_rec_ln_beta, L0_rec_attn_w, L0_rec_attn_b)
    return y

_drawn_inputs = setup_inputs


def setup_inputs(seed=0):
    import zlib

    import numpy as np

    out = dict(_drawn_inputs(seed))
    spreads = {'L0_rec_bn_gamma': (1.0, 0.2),
     'L0_rec_bn_beta': (0.0, 0.1),
     'L0_rec_ln_gamma': (1.0, 0.2),
     'L0_rec_ln_beta': (0.0, 0.1)}
    factors = {'L0_rec_masker_param': 4.958,
     'L0_rec_masker_bias': 8.0,
     'L0_rec_b_ih': 5.531,
     'L0_rec_b_hh': 5.806}
    for name, (base, spread) in spreads.items():
        noise = np.random.default_rng([zlib.crc32(name.encode()), seed]).standard_normal(out[name].shape)
        drawn = base * np.exp(spread * noise) if base else spread * noise
        out[name] = jnp.asarray(drawn.astype(out[name].dtype))
    for name, factor in factors.items():
        out[name] = (out[name] * factor).astype(out[name].dtype)
    return out
```

```python
import concourse.bass as bass
from concourse import mybir
from contextlib import ExitStack

fp32 = mybir.dt.float32
fp32r = mybir.dt.float32r
ALU = mybir.AluOpType
ACT = mybir.ActivationFunctionType
AX = mybir.AxisListType

B, N, D, T = 2048, 50, 32, 2
TN = T * N
P = 128
TILES = B // P
KX = N * D
KROWS = KX + 1
KC = (KROWS + P - 1) // P
KLAST = KROWS - (KC - 1) * P
GN = 10
GW = GN * N
GROUPS = T * N // GN
BLK = 8
BLOCKS = TILES // BLK
ITERS = BLOCKS * GROUPS
MPAD = 64
PAIRS = GN // 2
EPS_ROW = 1e-6
EPS = 1e-5
UNITS = [(u, min(u + 2, KC)) for u in range(0, KC, 2)]
NU = len(UNITS)
T_AT = 3

BANK = 512

QB = 4
ROUNDS = 32 // QB
RC = QB * TN
R_G, Z_G, N_G = 0, 1, 2


def wait(eng, sem, value):
    if not (isinstance(value, int) and value <= 0):
        eng.wait_ge(sem, value)


def stage1(nc, psum, xT, W, adjT, ident_d):
    with ExitStack() as ctx:
        sb = lambda name, shape, dt=fp32: ctx.enter_context(nc.sbuf_tensor(name, shape, dt))
        sem = lambda name: ctx.enter_context(nc.semaphore(name))
        x_hi = sb("x_hi", [P, KC, BLK * P], fp32r)
        x_lo = sb("x_lo", [P, KC, BLK * P], fp32r)
        x_raw = sb("x_raw", [P, KC, P])
        w_hi = sb("w_hi", [P, KC, GW], fp32r)
        w_lo = sb("w_lo", [P, KC, GW], fp32r)
        w_raw = sb("w_raw", [P, KC, GW])
        ident = sb("ident_sb", [P, P])
        u = sb("u", [P, 2, GN, N])
        an = sb("an", [P, 2, PAIRS, 2, MPAD])
        rows = sb("rows", [P, 3, GN])
        at = sb("at", [P, 2, PAIRS, P])

        x_loaded, ident_loaded = sem("x_loaded"), sem("ident_loaded")
        w_loaded = [sem(f"w_loaded{i}") for i in range(NU)]
        x_hi_ready, x_ready = sem("x_hi_ready"), sem("x_ready")
        w_hi_ready, w_ready, w_used = sem("w_hi_ready"), sem("w_ready"), sem("w_used")
        mm_done, u_ready, an_ready = sem("mm_done"), sem("u_ready"), sem("an_ready")
        tr_done, at_ready = sem("tr_done"), sem("at_ready")
        at_stored = [sem("at_stored0"), sem("at_stored1")]
        pad_zeroed, dve_step = sem("pad_zeroed"), sem("dve_step")

        def mm_out(c2):
            return psum[:, c2 * BANK:c2 * BANK + GW]

        def tr_out(c2):
            return psum[:, (2 + 2 * c2) * BANK:(2 + 2 * c2) * BANK + PAIRS * P]

        xT_main = xT[0:(KC - 1) * P, :].rearrange("(k p) b -> p k b", p=P)
        W_main = W[0:(KC - 1) * P, :].rearrange("(k p) n -> p k n", p=P)
        block = ctx.enter_context(nc.Block())

        @block.sync
        def _(sp):
            def load_x(bt):
                if bt >= 1:
                    sp.wait_ge(x_ready, bt)
                sp.dma_start(x_raw[:, 0:KC - 1, :], xT_main[:, :, bt * P:(bt + 1) * P]).then_inc(x_loaded, 16)
                sp.dma_start(x_raw[0:KLAST, KC - 1, :],
                             xT[(KC - 1) * P:KROWS, bt * P:(bt + 1) * P]).then_inc(x_loaded, 16)

            def load_w(i, group, after):
                k0, k1 = UNITS[i]
                if after is not None:
                    sp.wait_ge(w_ready, after)
                cols = bass.ds(group * GW, GW)
                if k1 < KC:
                    sp.dma_start(w_raw[:, k0:k1, :], W_main[:, k0:k1, cols]).then_inc(w_loaded[i], 16)
                else:
                    sp.dma_start(w_raw[0:KLAST, k0, :], W[(KC - 1) * P:KROWS, cols]).then_inc(w_loaded[i], 16)

            def store_tile(c, c2, tile, group):
                sp.wait_ge(at_ready, c + 1)
                for half in range(2):
                    sp.dma_start(adjT[tile, :, bass.ds(group * GN + half * PAIRS, PAIRS), :],
                                 at[MPAD * half:MPAD * half + N, c2, :, :]).then_inc(at_stored[c2], 16)

            load_x(0)
            for i in range(NU):
                load_w(i, 0, None)
            sp.dma_start(ident[:, :], ident_d).then_inc(ident_loaded, 16)
            for blk in range(BLOCKS):
                for it, group in p1_iters(sp, blk):
                    for w in range(BLK):
                        if isinstance(it, int) and it == 0 and w + 1 < BLK:
                            load_x(w + 1)
                        if w == 1 and not (isinstance(it, int) and it == ITERS - 1):
                            nxt = 0 if isinstance(it, int) and it % GROUPS == GROUPS - 1 else group + 1
                            for i in range(NU):
                                load_w(i, nxt, it * NU + i + 1)
                        c = it * BLK + w
                        if w > 0:
                            store_tile(c - 1, (w - 1) % 2, blk * BLK + w - 1, group)
                        elif not (isinstance(it, int) and it == 0):
                            if isinstance(it, int) and it % GROUPS == 0:
                                store_tile(c - 1, 1, blk * BLK - 1, GROUPS - 1)
                            else:
                                store_tile(c - 1, 1, blk * BLK + BLK - 1, group - 1)
                        if isinstance(it, int) and it == GROUPS - 1 and blk + 1 < BLOCKS and w >= 1:
                            load_x(BLK + w - 1)
                    if isinstance(it, int) and it == GROUPS - 1 and blk + 1 < BLOCKS:
                        load_x(2 * BLK - 1)
            store_tile(ITERS * BLK - 1, 1, TILES - 1, GROUPS - 1)
            sp.wait_ge(at_stored[0], 32 * (ITERS * BLK // 2))
            sp.wait_ge(at_stored[1], 32 * (ITERS * BLK // 2))

        def split_x_hi(act, bt):
            act.wait_ge(x_loaded, 32 * (bt + 1))
            if bt >= BLK:
                act.wait_ge(mm_done, (GROUPS - 1) * BLK + bt - BLK + 1)
            cols = bass.ts(bt % BLK, P)
            nc.scalar.copy(x_hi[:, 0:KC - 1, cols], x_raw[:, 0:KC - 1, :])
            nc.scalar.copy(x_hi[0:KLAST, KC - 1, cols], x_raw[0:KLAST, KC - 1, :]).then_inc(x_hi_ready, 1)

        def split_x_lo(dve, bt):
            dve.wait_ge(x_hi_ready, bt + 1)
            cols = bass.ts(bt % BLK, P)
            for rows_, ks in ((P, slice(0, KC - 1)), (KLAST, slice(KC - 1, KC))):
                last = nc.vector.tensor_tensor(x_lo[0:rows_, ks, cols], x_raw[0:rows_, ks, :],
                                               x_hi[0:rows_, ks, cols].bitcast(fp32), ALU.subtract)
            last.then_inc(x_ready, 1)

        def split_w_hi(act, i, it):
            act.wait_ge(w_loaded[i], (it + 1) * 16)
            if not (isinstance(it, int) and it == 0):
                if i == NU - 1:
                    act.wait_ge(mm_done, it * BLK)
                else:
                    act.wait_ge(w_used, (it - 1) * (NU - 1) + i + 1)
            k0, k1 = UNITS[i]
            r = P if k1 < KC else KLAST
            nc.scalar.copy(w_hi[0:r, k0:k1, :], w_raw[0:r, k0:k1, :]).then_inc(w_hi_ready, 1)

        def split_w_lo(dve, i, it):
            dve.wait_ge(w_hi_ready, it * NU + i + 1)
            k0, k1 = UNITS[i]
            r = P if k1 < KC else KLAST
            nc.vector.tensor_tensor(w_lo[0:r, k0:k1, :], w_raw[0:r, k0:k1, :],
                                    w_hi[0:r, k0:k1, :].bitcast(fp32), ALU.subtract).then_inc(w_ready, 1)

        @block.scalar
        def _(act):
            def relu(c, c2, start=False):
                act.wait_ge(mm_done, c + 1)
                if not start:
                    act.wait_ge(an_ready, c - 1)
                nc.scalar.activation(u[:, c2].rearrange("p n m -> p (n m)"), mm_out(c2), ACT.Relu).then_inc(u_ready, 1)

            def evacuate(c, c2, start=False):
                act.wait_ge(tr_done, c + 1)
                if not start:
                    act.wait_ge(at_stored[c2], 16 * (c - c2))
                nc.scalar.copy(at[:, c2].rearrange("p q b -> p (q b)"), tr_out(c2)).then_inc(at_ready, 1)

            split_x_hi(act, 0)
            for i in range(NU):
                split_w_hi(act, i, 0)
            for blk in range(BLOCKS):
                for it, group in p1_iters(act, blk):
                    static = isinstance(it, int)
                    for w in range(BLK):
                        c = it * BLK + w
                        split = w == BLK - 1 and not (static and it == ITERS - 1)
                        if not (static and it == 0 and w == 0):
                            relu(c - 1, (w - 1) % 2, start=static and it == 0 and w <= 2)
                        if static and it == 0 and w + 1 < BLK:
                            split_x_hi(act, w + 1)
                        if split:
                            for i in range(0, T_AT + 1):
                                split_w_hi(act, i, it + 1)
                        if not (static and it == 0 and w == 0):
                            evacuate(c - 1, (w - 1) % 2, start=static and it == 0 and w <= 2)
                        if split:
                            for i in range(T_AT + 1, NU):
                                split_w_hi(act, i, it + 1)
                        if static and it == GROUPS - 1 and w >= 1:
                            split_x_hi(act, BLK + w - 1)
                    if static and it == GROUPS - 1:
                        split_x_hi(act, 2 * BLK - 1)
            c = ITERS * BLK - 1
            relu(c, 1)
            evacuate(c, 1)

        @block.vector
        def _(dve):
            nc.vector.memset(an[:].rearrange("p c q h m -> p (c q h m)"), 0.0).then_inc(pad_zeroed, 1)
            dve.wait_ge(pad_zeroed, 1)

            def normalise(c, c2, start=False):
                dve.wait_ge(u_ready, c + 1)
                nc.vector.tensor_reduce(rows[:, 0], u[:, c2], AX.X, ALU.add).then_inc(dve_step, 1)
                dve.wait_ge(dve_step, 3 * c + 1)
                nc.vector.tensor_scalar_add(rows[:, 1], rows[:, 0], EPS_ROW).then_inc(dve_step, 1)
                dve.wait_ge(dve_step, 3 * c + 2)
                nc.vector.reciprocal(rows[:, 2], rows[:, 1]).then_inc(dve_step, 1)
                dve.wait_ge(dve_step, 3 * c + 3)
                if not start:
                    dve.wait_ge(tr_done, c - 1)
                nc.vector.tensor_tensor(an[:, c2, :, :, 0:N].rearrange("p q h m -> p h q m"),
                                        u[:, c2].rearrange("p (h q) m -> p h q m", h=2),
                                        rows[:, 2].rearrange("p (h q) -> p h q", h=2).unsqueeze(3).to_broadcast([P, 2, PAIRS, N]),
                                        ALU.mult).then_inc(an_ready, 1)

            split_x_lo(dve, 0)
            for i in range(NU):
                split_w_lo(dve, i, 0)
            for blk in range(BLOCKS):
                for it, group in p1_iters(dve, blk):
                    static = isinstance(it, int)
                    for w in range(BLK):
                        c = it * BLK + w
                        if not (static and it == 0 and w == 0):
                            normalise(c - 1, (w - 1) % 2, start=static and it == 0 and w <= 2)
                        if static and it == 0 and w + 1 < BLK:
                            split_x_lo(dve, w + 1)
                        if w == BLK - 1 and not (static and it == ITERS - 1):
                            for i in range(NU):
                                split_w_lo(dve, i, it + 1)
                        if static and it == GROUPS - 1 and w >= 1:
                            split_x_lo(dve, BLK + w - 1)
                    if static and it == GROUPS - 1:
                        split_x_lo(dve, 2 * BLK - 1)
            normalise(ITERS * BLK - 1, 1)

        @block.tensor
        def _(pe):
            def transposes(c, c2, start=False):
                pe.wait_ge(an_ready, c + 1)
                if not start:
                    pe.wait_ge(at_ready, c - 1)
                for q in range(PAIRS):
                    last = nc.tensor.transpose(tr_out(c2)[:, q * P:(q + 1) * P],
                                               an[:, c2, q].rearrange("p h m -> p (h m)"), ident[:, :])
                last.then_inc(tr_done, 1)

            def window(it, w, blk, c, start=False, bank_free=False, none_before=False):
                pe.wait_ge(x_ready, blk * BLK + w + 1)
                if not bank_free:
                    pe.wait_ge(u_ready, c - 1)
                cols = bass.ts(w, P)
                for i, (k0, k1) in enumerate(UNITS):
                    if w == 0:
                        pe.wait_ge(w_ready, it * NU + i + 1)
                    for k in range(k0, k1):
                        r = P if k < KC - 1 else KLAST
                        for n, (a, b) in enumerate(((x_lo, w_hi), (x_hi, w_lo), (x_hi, w_hi))):
                            last = nc.tensor.matmul(mm_out(w % 2), a[0:r, k, cols], b[0:r, k, :],
                                                    start=(k == 0 and n == 0), stop=(k == KC - 1 and n == 2))
                    if i == NU - 1:
                        last.then_inc(mm_done, 1)
                    elif w == BLK - 1:
                        last.then_inc(w_used, 1)
                    if i == T_AT and not none_before:
                        transposes(c - 1, (w - 1) % 2, start=start)

            pe.wait_ge(ident_loaded, 16)
            for blk in range(BLOCKS):
                for it, group in pe_iters(pe, blk):
                    static = isinstance(it, int)
                    for w in range(BLK):
                        c = it * BLK + w
                        window(it, w, blk, c, start=static and it == 0 and w <= 2,
                               bank_free=static and it == 0 and w < 2, none_before=static and it == 0 and w == 0)
            transposes(ITERS * BLK - 1, 1)


def p1_iters(eng, blk):
    base = blk * GROUPS
    yield base, 0
    with eng.Fori(1, GROUPS - 1) as g:
        yield base + g, g
    yield base + GROUPS - 1, GROUPS - 1


def pe_iters(eng, blk):
    base = blk * GROUPS
    if blk == 0:
        yield 0, 0
    with eng.Fori(1 if blk == 0 else 0, GROUPS) as g:
        yield base + g, g


def stage2(nc, psum, ins, adjT, hB, stats):
    with ExitStack() as ctx:
        sb = lambda name, shape, dt=fp32: ctx.enter_context(nc.sbuf_tensor(name, shape, dt))
        sem = lambda name: ctx.enter_context(nc.semaphore(name))
        adj = sb("adj_sb", [P, TN, P])
        xs = sb("xs_sb", [P, P, D])
        xg = sb("xg_sb", [P, 2, 32, N])
        xg_hi = sb("xg_hi", [P, 2, 32, N], fp32r)
        xg_lo = sb("xg_lo", [P, 2, 32, N], fp32r)
        hG = sb("hG", [P, 2, 32, TN])
        hT = sb("hT", [P, TN, D])
        dev = sb("dev", [P, 32, TN])
        m_hi = sb("m_hi", [P, 2, RC], fp32r)
        m_lo = sb("m_lo", [P, 2, RC], fp32r)
        r_gate = sb("r_gate", [P, 2, RC])
        z_gate = sb("z_gate", [P, 2, RC])
        n_in = sb("n_in", [P, 2, RC])
        n_gate = sb("n_gate", [P, 2, RC])
        diff = sb("diff", [P, RC])
        tile_sum = sb("tile_sum", [P, 2, TN])
        wT4 = sb("wT4_sb", [D, P])
        wih = sb("wih_sb", [D, 3 * D])
        whh4 = sb("whh_sb", [P, 3 * D])
        biases = sb("biases_sb", [P, 2, 3])
        bias = sb("bias", [P, 3])
        wd = sb("wd", [P, 2, 3, P])
        wd_hi = sb("wd_hi", [P, 2, 3, P], fp32r)
        wd_lo = sb("wd_lo", [P, 2, 3, P], fp32r)
        means, devs = stats

        consts_loaded, g_product, zeroed, blocks_ready = sem("consts_loaded"), sem("g_product"), sem("zeroed"), sem("blocks_ready")
        wd_hi_ready, wd_ready, bias_ready = sem("wd_hi_ready"), sem("wd_ready"), sem("bias_ready")
        adj_loaded = [sem("adj_loaded0"), sem("adj_loaded1")]
        xg_loaded = [sem("xg_loaded0"), sem("xg_loaded1")]
        xg_hi_ready, xg_ready = sem("xg_hi_ready"), sem("xg_ready")
        ax_done, m_hi_ready, m_ready = sem("ax_done"), sem("m_hi_ready"), sem("m_ready")
        gate_done = [sem(f"{g}_done") for g in ("r", "z", "n")]
        r_ready, z_ready, n_in_ready, n_ready = sem("r_ready"), sem("z_ready"), sem("n_in_ready"), sem("n_ready")
        d_step, h_ready = sem("d_step"), sem("h_ready")
        hT_ready, hT_stored, sum_ready = sem("hT_ready"), sem("hT_stored"), sem("sum_ready")
        pool_step, d_sum = sem("pool_step"), sem("d_sum")
        hG_read = [sem("hG_read0"), sem("hG_read1")]

        S = 2 * ROUNDS
        ax_bank = lambda s: psum[:, (s % 2) * BANK:(s % 2) * BANK + RC]
        gate_bank = lambda gate, s: psum[:, (2 + 2 * gate + s % 2) * BANK:(2 + 2 * gate + s % 2) * BANK + RC]
        block = ctx.enter_context(nc.Block())

        @block.sync
        def _(sp):
            def load_adj(tile, r):
                sp.dma_start(adj[MPAD * r:MPAD * r + N, :, :], adjT[tile]).then_inc(adj_loaded[r], 16)
                sp.dma_start(xs[MPAD * r:MPAD * r + N, :, :],
                             ins["xm"][:, bass.ds(tile * P, P), :]).then_inc(adj_loaded[r], 16)

            def load_xg(tile, r):
                sp.dma_start(xg[:, r], ins["xg"][tile]).then_inc(xg_loaded[r], 16)

            def iteration(it, more):
                for r in range(2):
                    tile = it * 2 + r
                    if more:
                        sp.wait_ge(ax_done, (tile + 1) * ROUNDS)
                        load_adj(tile + 2, r)
                    sp.wait_ge(hT_ready, tile + 1)
                    sp.dma_start(hB[tile], hT[:]).then_inc(hT_stored, 16)
                    if more:
                        load_xg(tile + 2, r)

            for r in range(2):
                load_adj(r, r)
                load_xg(r, r)
            for dst, src in ((wT4, "wT4"), (wih, "wihT"), (whh4, "whhT4"), (biases, "biases")):
                sp.dma_start(dst[:], ins[src]).then_inc(consts_loaded, 16)
            with sp.Fori(0, TILES // 2 - 1) as it:
                iteration(it, True)
            iteration(TILES // 2 - 1, False)
            sp.wait_ge(hT_stored, 16 * TILES)

        @block.scalar
        def _(act):
            act.wait_ge(blocks_ready, 1)
            nc.scalar.copy(wd_hi[:], wd[:]).then_inc(wd_hi_ready, 1)
            act.wait_ge(bias_ready, 1)

            def x_hi(it, r):
                act.wait_ge(xg_loaded[r], (it + 1) * 16)
                if r == 1:
                    wait(act, gate_done[Z_G], it * S)
                else:
                    wait(act, gate_done[Z_G], it * S - ROUNDS)
                nc.scalar.copy(xg_hi[:, r], xg[:, r]).then_inc(xg_hi_ready, 1)

            def m_halves(it, s):
                act.wait_ge(ax_done, it * S + s + 1)
                nc.scalar.copy(m_hi[:, s % 2], ax_bank(s)).then_inc(m_hi_ready, 1)

            def turn(it, more):
                for s in range(S):
                    if s + 1 < S or more:
                        wait(act, gate_done[Z_G], it * S + s)
                        m_halves(it + (s + 1) // S, (s + 1) % S)
                    if s == ROUNDS - 3:
                        x_hi(it, 1)
                    if s == S - 3 and more:
                        x_hi(it + 1, 0)
                    act.wait_ge(gate_done[R_G], it * S + s + 1)
                    wait(act, h_ready, it * S + s - 1)
                    nc.scalar.activation(r_gate[:, s % 2], gate_bank(R_G, s), ACT.Sigmoid,
                                         bias=bias[:, R_G:R_G + 1]).then_inc(r_ready, 1)
                    act.wait_ge(gate_done[Z_G], it * S + s + 1)
                    nc.scalar.activation(z_gate[:, s % 2], gate_bank(Z_G, s), ACT.Sigmoid,
                                         bias=bias[:, Z_G:Z_G + 1]).then_inc(z_ready, 1)
                    act.wait_ge(n_in_ready, it * S + s + 1)
                    nc.scalar.activation(n_gate[:, s % 2], n_in[:, s % 2], ACT.Tanh).then_inc(n_ready, 1)

            x_hi(0, 0)
            m_halves(0, 0)
            turn(0, True)
            with act.Fori(1, TILES // 2 - 1) as it:
                turn(it, True)
            turn(TILES // 2 - 1, False)

        @block.vector
        def _(dve):
            nc.vector.memset(wd[:], 0.0).then_inc(zeroed, 1)
            dve.wait_ge(zeroed, 1)
            dve.wait_ge(consts_loaded, 64)
            dve.wait_ge(g_product, 1)
            for j in range(4):
                q = slice(D * j, D * j + D)
                nc.vector.tensor_copy(wd[q, 0, :, q], psum[q, 0:3 * D].rearrange("p (g e) -> p g e", g=3))
                last = nc.vector.tensor_copy(wd[q, 1, :, q], whh4[q, :].rearrange("p (g e) -> p g e", g=3))
            last.then_inc(blocks_ready, 1)
            nc.vector.tensor_tensor(bias[:], biases[:, 0], biases[:, 1], ALU.add).then_inc(bias_ready, 1)
            dve.wait_ge(wd_hi_ready, 1)
            nc.vector.tensor_tensor(wd_lo[:], wd[:], wd_hi[:].bitcast(fp32), ALU.subtract).then_inc(wd_ready, 1)
            dve.wait_ge(bias_ready, 1)
            def x_lo(it, r):
                dve.wait_ge(xg_hi_ready, it * 2 + r + 1)
                nc.vector.tensor_tensor(xg_lo[:, r], xg[:, r], xg_hi[:, r].bitcast(fp32),
                                        ALU.subtract).then_inc(xg_ready, 1)

            def m_halves(it, s):
                dve.wait_ge(m_hi_ready, it * S + s + 1)
                nc.vector.tensor_tensor(m_lo[:, s % 2], ax_bank(s), m_hi[:, s % 2].bitcast(fp32),
                                        ALU.subtract).then_inc(m_ready, 1)

            def nodes(ap):
                return ap.rearrange("p (g t n) -> p g t n", g=QB, t=T)

            def update(it, s):
                r, q = divmod(s, ROUNDS)
                base = (it * S + s) * 2
                dve.wait_ge(gate_done[N_G], it * S + s + 1)
                dve.wait_ge(r_ready, it * S + s + 1)
                nc.vector.scalar_tensor_tensor(out=n_in[:, s % 2], in0=gate_bank(N_G, s), scalar=bias[:, N_G:N_G + 1],
                                               in1=r_gate[:, s % 2], op0=ALU.add, op1=ALU.mult).then_inc(n_in_ready, 1)

            def finish(it, s):
                r, q = divmod(s, ROUNDS)
                base = (it * S + s) * 2
                dve.wait_ge(n_ready, it * S + s + 1)
                x_b = xg[:, r, q * QB:(q + 1) * QB, :].unsqueeze(2).to_broadcast([P, QB, T, N])
                nc.vector.tensor_tensor(nodes(diff[:]), x_b, nodes(n_gate[:, s % 2]), ALU.subtract).then_inc(d_step, 1)
                dve.wait_ge(d_step, base + 1)
                dve.wait_ge(z_ready, it * S + s + 1)
                nc.vector.tensor_tensor(diff[:], diff[:], z_gate[:, s % 2], ALU.mult).then_inc(d_step, 1)
                dve.wait_ge(d_step, base + 2)
                nc.vector.tensor_tensor(hG[:, r, q * QB:(q + 1) * QB, :].rearrange("p g c -> p (g c)"), diff[:],
                                        n_gate[:, s % 2], ALU.add).then_inc(h_ready, 1)

            def tile_end(it, r):
                tile = it * 2 + r
                dve.wait_ge(h_ready, it * S + (r + 1) * ROUNDS)
                wait(dve, hT_stored, 16 * tile)
                by_row = hG[:, r].rearrange("p g c -> p c g")
                nc.vector.transpose(hT[:], by_row).then_inc(hT_ready, 1)
                nc.vector.tensor_reduce(tile_sum[:, r], by_row, AX.X, ALU.add).then_inc(d_sum, 1)
                dve.wait_ge(d_sum, tile + 1)
                nc.vector.tensor_scalar(means[:, bass.ds(tile, 1), :], tile_sum[:, r:r + 1], 1.0 / 32, None,
                                        ALU.mult).then_inc(sum_ready, 1)

            def turn(it, more):
                for s in range(S):
                    if s + 1 < S or more:
                        m_halves(it + (s + 1) // S, (s + 1) % S)
                    if s == ROUNDS - 3:
                        x_lo(it, 1)
                    if s == S - 3 and more:
                        x_lo(it + 1, 0)
                    update(it, s)
                    if s % ROUNDS == 0:
                        wait(dve, hG_read[s // ROUNDS], it)
                    finish(it, s)
                    if s % ROUNDS == ROUNDS - 1:
                        tile_end(it, s // ROUNDS)

            x_lo(0, 0)
            m_halves(0, 0)
            turn(0, True)
            with dve.Fori(1, TILES // 2 - 1) as it:
                turn(it, True)
            turn(TILES // 2 - 1, False)

        @block.gpsimd
        def _(pool):
            with pool.Fori(0, TILES // 2) as it:
                for r in range(2):
                    tile = it * 2 + r
                    step = tile * 6
                    mean = means[:, bass.ds(tile, 1), :]
                    pool.wait_ge(sum_ready, tile + 1)
                    nc.gpsimd.tensor_tensor(dev[:], hG[:, r], mean.to_broadcast([P, 32, TN]),
                                            ALU.subtract).then_inc(hG_read[r], 1)
                    pool.wait_ge(hG_read[r], it + 1)
                    nc.gpsimd.tensor_tensor(dev[:], dev[:], dev[:], ALU.mult).then_inc(pool_step, 1)
                    for n, g in enumerate((16, 8, 4, 2)):
                        pool.wait_ge(pool_step, step + n + 1)
                        nc.gpsimd.tensor_tensor(dev[:, 0:g], dev[:, 0:g], dev[:, g:2 * g], ALU.add).then_inc(pool_step, 1)
                    pool.wait_ge(pool_step, step + 5)
                    nc.gpsimd.tensor_tensor(devs[:, bass.ds(tile, 1), :], dev[:, 0:1], dev[:, 1:2],
                                            ALU.add).then_inc(pool_step, 1)
                    pool.wait_ge(pool_step, step + 6)

        @block.tensor
        def _(pe):
            pe.wait_ge(consts_loaded, 64)
            nc.tensor.matmul(psum[:, 0:3 * D], wT4[:], wih[:], start=True, stop=True).then_inc(g_product, 1)
            pe.wait_ge(wd_ready, 1)

            def aggregate(s):
                r, q = divmod(s, ROUNDS)
                rows = slice(MPAD * r, MPAD * r + N)
                for gi in range(QB):
                    for j in range(4):
                        b = 32 * j + q * QB + gi
                        last = nc.tensor.matmul(ax_bank(s)[D * j:D * j + D, gi * TN:(gi + 1) * TN],
                                                xs[rows, b, :], adj[rows, :, b], start=True, stop=True)
                last.then_inc(ax_done, 1)

            def gates(it, s, more):
                r, q = divmod(s, ROUNDS)
                if q == 0:
                    pe.wait_ge(xg_ready, it * 2 + r + 1)
                if s == ROUNDS - 2:
                    pe.wait_ge(adj_loaded[1], (it + 1) * 32)
                if s == S - 2 and more:
                    pe.wait_ge(adj_loaded[0], (it + 2) * 32)
                pe.wait_ge(m_ready, it * S + s + 1)
                xb = [t[:, r, q * QB:(q + 1) * QB, :].unsqueeze(2).to_broadcast([P, QB, T, N]) for t in (xg_hi, xg_lo)]
                for gate in (R_G, N_G, Z_G):
                    free = (r_ready, z_ready, n_in_ready)[gate]
                    wait(pe, free, it * S + s - 1)
                    terms = []
                    for part, (hi, lo) in enumerate(((m_hi[:, s % 2], m_lo[:, s % 2]), xb)):
                        terms += [(wd_lo[:, part, gate], hi), (wd_hi[:, part, gate], lo), (wd_hi[:, part, gate], hi)]
                    for i, (w, m) in enumerate(terms):
                        last = nc.tensor.matmul(gate_bank(gate, s), w, m, start=i == 0, stop=i == len(terms) - 1)
                    last.then_inc(gate_done[gate], 1)

            def turn(it, more):
                for s in range(S):
                    if s + 1 < S or more:
                        aggregate((s + 1) % S)
                    gates(it, s, more)

            pe.wait_ge(adj_loaded[0], 32)
            aggregate(0)
            turn(0, True)
            with pe.Fori(1, TILES // 2 - 1) as it:
                turn(it, True)
            turn(TILES // 2 - 1, False)


def stage3(nc, psum, ins, hB, rows_d, stats, out):
    F = TN * D
    with ExitStack() as ctx:
        sb = lambda name, shape, dt=fp32: ctx.enter_context(nc.sbuf_tensor(name, shape, dt))
        sem = lambda name: ctx.enter_context(nc.semaphore(name))
        means, devs = stats
        ident = sb("ident3_sb", [P, P])
        fold = sb("fold_sb", [P, P])
        gamma = sb("gamma_sb", [D, TN])
        beta = sb("beta_sb", [D, TN])
        acc = sb("acc", [P, 5, P])
        mdev = sb("mdev", [P, TILES, TN])
        bn = sb("bn", [D, 2, P])
        bn_rows = sb("bn_rows", [D, 2, 4, D])
        A = sb("A_row", [P, TN, D])
        C = sb("C_row", [P, TN, D])
        LG = sb("LG_row", [P, TN, D])
        LA = sb("LA_row", [P, TN, D])
        aw = sb("aw_sb", [P, D])
        ab = sb("ab_sb", [P, 1])
        K1 = sb("K1", [P, TN])
        K2 = sb("K2", [P, TN])
        LGt = sb("LGt", [TN, T, D])
        LBt = sb("LBt", [TN, T, D])
        eps = sb("eps", [P, 1])
        h = sb("h_sb", [P, 2, TN, D])
        z = sb("z_sb", [P, 2, TN, D])
        v = sb("v_sb", [P, TN, D])
        pr = sb("pr_sb", [P, 2, TN, D])
        sq = sb("sq_sb", [P, TN, D])
        col = sb("col", [P, 2, 5])
        q = sb("q_sb", [P, TN])
        sc = sb("sc", [P, 2, T, N])
        ex = sb("ex", [P, T, N])
        mx = sb("mx", [P, 3, T])
        w = sb("w_sb", [P, 2, TN])
        ww = sb("ww_sb", [P, 2, TN])
        wT = sb("wT_sb", [TN, 2, P])
        pooled = sb("pooled", [P, T, D])
        res = sb("res_sb", [P, 2, T * D])

        loaded, ones_set, st = sem("loaded"), sem("ones_set"), sem("st")
        folded, dev_sqrt, bn_stored, rows_loaded = sem("folded"), sem("dev_sqrt"), sem("bn_stored"), sem("rows_loaded")
        lb_used = sem("lb_used")
        h_loaded = [sem("h_loaded0"), sem("h_loaded1")]
        y_ready, z_ready, m_ready, sq_ready, std_ready = sem("y_ready"), sem("z3_ready"), sem("nm_ready"), sem("sq_ready"), sem("std_ready")
        v_ready, p_ready, q_ready = sem("v_ready"), sem("p_ready"), sem("q_ready")
        sc_step, shifted, exp_ready, w_ready = sem("sc_step"), sem("shifted"), sem("exp_ready"), sem("w3_ready")
        wT_done, wT_ready, corr_done = sem("wT_done"), sem("wT_ready"), sem("corr_done")
        pw_ready, pooled_ready, res_ready = sem("pw_ready"), sem("pooled_ready"), sem("res_ready")
        stored = [sem("stored0"), sem("stored1")]
        block = ctx.enter_context(nc.Block())
        flat = lambda ap: ap.rearrange("p c d -> p (c d)")
        corr_bank = psum[:, 4 * BANK:4 * BANK + T * D]

        @block.sync
        def _(sp):
            sp.wait_ge(ones_set, 1)
            loads = [(ident[:], ins["ident"]), (fold[:], ins["fold"]), (gamma[:], ins["bn_gamma"]), (beta[:], ins["bn_beta"]),
                     (LG[:], ins["ln_gamma"].partition_broadcast(P)), (C[:], ins["ln_beta"].partition_broadcast(P)),
                     (aw[:], ins["attn_w"].partition_broadcast(P)), (ab[:], ins["attn_b"].partition_broadcast(P))]
            for t in range(T):
                loads += [(LGt[t * N:t * N + N, t, :], ins["ln_gamma"][t * N:t * N + N, :]),
                          (LBt[t * N:t * N + N, t, :], ins["ln_beta"][t * N:t * N + N, :])]
            assert len(loads) == N_LOADS
            for dst, src in loads:
                sp.dma_start(dst, src).then_inc(loaded, 16)
            for p in range(2):
                sp.dma_start(h[:, p], hB[p]).then_inc(h_loaded[p], 16)
            sp.wait_ge(st, ST_ROWS)
            for i in range(2):
                sp.dma_start(rows_d[i, 0:96, :].rearrange("(k p) d -> p k d", p=D), bn_rows[:, i, 0:3, :]).then_inc(bn_stored, 16)
                sp.dma_start(rows_d[i, 96:TN, :], bn_rows[0:TN - 96, i, 3, :]).then_inc(bn_stored, 16)
            sp.wait_ge(bn_stored, 64)
            sp.dma_start(A[:], rows_d[0].partition_broadcast(P)).then_inc(rows_loaded, 16)
            sp.wait_ge(lb_used, 1)
            sp.dma_start(C[:], rows_d[1].partition_broadcast(P)).then_inc(rows_loaded, 16)

            def tile_io(tile, p, more):
                if more:
                    sp.wait_ge(z_ready, tile + 1)
                    sp.dma_start(h[:, p], hB[tile + 2]).then_inc(h_loaded[p], 16)
                sp.wait_ge(res_ready, tile + 1)
                sp.dma_start(out[tile], res[:, p]).then_inc(stored[p], 16)
            with sp.Fori(0, TILES // 2 - 1) as it:
                for p in range(2):
                    tile_io(it * 2 + p, p, True)
            for p in range(2):
                tile_io(TILES - 2 + p, p, False)
            for p in range(2):
                sp.wait_ge(stored[p], 16 * (TILES // 2))

        def pipeline(eng, first, second):
            def turn(it):
                first(it * 2 + 1, 1, it)
                second(it * 2, 0, it)
                first(it * 2 + 2, 0, it + 1)
                second(it * 2 + 1, 1, it)
            first(0, 0, 0)
            turn(0)
            with eng.Fori(1, TILES // 2 - 1) as it:
                turn(it)
            last = TILES // 2 - 1
            first(TILES - 1, 1, last)
            second(TILES - 2, 0, last)
            second(TILES - 1, 1, last)

        @block.vector
        def _(dve):
            n = [0]

            def step(ins_):
                n[0] += 1
                ins_.then_inc(st, 1)
                dve.wait_ge(st, n[0])

            step(nc.vector.memset(LGt[:], 0.0))
            step(nc.vector.memset(eps[:], EPS))
            step(nc.vector.memset(bn[:], 0.0))
            nc.vector.memset(LBt[:], 0.0).then_inc(ones_set, 1)
            dve.wait_ge(ones_set, 1)
            dve.wait_ge(loaded, 16 * N_LOADS)
            by_node = lambda ap: ap.rearrange("p i c -> p c i")
            step(nc.vector.tensor_reduce(acc[:, 0, 0:TN], by_node(means[:]), AX.X, ALU.add))
            dve.wait_ge(folded, 1)
            step(nc.vector.tensor_scalar(acc[:, 1, 0:TN], psum[:, 0:TN], 1.0 / (4 * TILES), None, ALU.mult))
            step(nc.vector.tensor_tensor(mdev[:], means[:], acc[:, 1:2, 0:TN].to_broadcast([P, TILES, TN]), ALU.subtract))
            step(nc.vector.tensor_tensor(mdev[:], mdev[:], mdev[:], ALU.mult))
            step(nc.vector.scalar_tensor_tensor(out=mdev[:], in0=mdev[:], scalar=32.0, in1=devs[:], op0=ALU.mult, op1=ALU.add))
            step(nc.vector.tensor_reduce(acc[:, 2, 0:TN], by_node(mdev[:]), AX.X, ALU.add))
            assert n[0] == ST_VAR
            dve.wait_ge(dev_sqrt, 1)
            step(nc.vector.reciprocal(acc[0:D, 4, 0:TN], acc[0:D, 3, 0:TN]))
            step(nc.vector.tensor_tensor(bn[:, 0, 0:TN], gamma[:], acc[0:D, 4, 0:TN], ALU.mult))
            step(nc.vector.tensor_tensor(acc[0:D, 4, 0:TN], acc[0:D, 1, 0:TN], bn[:, 0, 0:TN], ALU.mult))
            step(nc.vector.tensor_tensor(bn[:, 1, 0:TN], beta[:], acc[0:D, 4, 0:TN], ALU.subtract))
            step(nc.vector.transpose(bn_rows[:].rearrange("p i k d -> p (i k d)"), bn[:].rearrange("p i c -> p (i c)")))
            assert n[0] == ST_ROWS
            step(nc.vector.tensor_tensor(LA[:], LG[:], aw[:].unsqueeze(1).to_broadcast([P, TN, D]), ALU.mult))
            step(nc.vector.tensor_reduce(K1[:], LA[:], AX.X, ALU.add))
            step(nc.vector.tensor_tensor(v[:], C[:], aw[:].unsqueeze(1).to_broadcast([P, TN, D]), ALU.mult))
            step(nc.vector.tensor_reduce(K2[:], v[:], AX.X, ALU.add))
            nc.vector.tensor_scalar(K2[:], K2[:], ab[:], None, ALU.add).then_inc(lb_used, 1)
            dve.wait_ge(lb_used, 1)
            dve.wait_ge(rows_loaded, 32)

            def norm(tile, p, it):
                dve.wait_ge(h_loaded[p], (it + 1) * 16)
                nc.vector.tensor_tensor(h[:, p], h[:, p], A[:], ALU.mult).then_inc(y_ready, 1)
                dve.wait_ge(y_ready, tile + 1)
                wait(dve, p_ready, it * 2)
                nc.vector.scalar_tensor_tensor(out=flat(z[:, p]), in0=flat(h[:, p]), scalar=1.0, in1=flat(C[:]), op0=ALU.mult,
                                               op1=ALU.add, accum_out=col[:, p, 0:1]).then_inc(z_ready, 1)
                dve.wait_ge(z_ready, tile + 1)
                nc.vector.tensor_scalar(col[:, p, 1:2], col[:, p, 0:1], -1.0 / F, None, ALU.mult).then_inc(m_ready, 1)

            def attend(tile, p, it):
                k = tile * 9
                dve.wait_ge(v_ready, tile + 1)
                nc.vector.tensor_reduce(q[:], v[:], AX.X, ALU.add).then_inc(q_ready, 1)
                dve.wait_ge(std_ready, tile + 1)
                nc.vector.reciprocal(col[:, p, 4:5], col[:, p, 3:4]).then_inc(sc_step, 1)
                dve.wait_ge(q_ready, tile + 1)
                nc.vector.scalar_tensor_tensor(out=sc[:, 0].rearrange("p t n -> p (t n)"), in0=K1[:], scalar=col[:, p, 1:2], in1=q[:],
                                               op0=ALU.mult, op1=ALU.add).then_inc(sc_step, 1)
                dve.wait_ge(sc_step, k + 2)
                nc.vector.scalar_tensor_tensor(out=sc[:, 1].rearrange("p t n -> p (t n)"), in0=sc[:, 0].rearrange("p t n -> p (t n)"),
                                               scalar=col[:, p, 4:5], in1=K2[:], op0=ALU.mult, op1=ALU.add).then_inc(sc_step, 1)
                dve.wait_ge(sc_step, k + 3)
                nc.vector.tensor_reduce(mx[:, 0], sc[:, 1], AX.X, ALU.max).then_inc(sc_step, 1)
                dve.wait_ge(sc_step, k + 4)
                nc.vector.tensor_tensor(sc[:, 0], sc[:, 1], mx[:, 0].unsqueeze(2).to_broadcast([P, T, N]), ALU.subtract).then_inc(shifted, 1)
                dve.wait_ge(exp_ready, tile + 1)
                nc.vector.tensor_reduce(mx[:, 1], ex[:], AX.X, ALU.add).then_inc(sc_step, 1)
                dve.wait_ge(sc_step, k + 5)
                nc.vector.reciprocal(mx[:, 2], mx[:, 1]).then_inc(sc_step, 1)
                dve.wait_ge(sc_step, k + 6)
                nc.vector.tensor_tensor(w[:, 0].rearrange("p (t n) -> p t n", t=T), ex[:], mx[:, 2].unsqueeze(2).to_broadcast([P, T, N]),
                                        ALU.mult).then_inc(sc_step, 1)
                dve.wait_ge(sc_step, k + 7)
                nc.vector.tensor_scalar(ww[:, 0], w[:, 0], col[:, p, 4:5], None, ALU.mult).then_inc(sc_step, 1)
                dve.wait_ge(sc_step, k + 8)
                nc.vector.tensor_scalar(w[:, 1], ww[:, 0], col[:, p, 1:2], None, ALU.mult).then_inc(w_ready, 1)
                dve.wait_ge(p_ready, tile + 1)
                nc.vector.tensor_tensor(pr[:, p], pr[:, p], ww[:, 0].unsqueeze(2).to_broadcast([P, TN, D]), ALU.mult).then_inc(pw_ready, 1)
                dve.wait_ge(pw_ready, tile + 1)
                nc.vector.tensor_reduce(pooled[:], pr[:, p].rearrange("p (t n) d -> p t d n", t=T), AX.X, ALU.add).then_inc(sc_step, 1)
                dve.wait_ge(sc_step, k + 9)
                dve.wait_ge(corr_done, tile + 1)
                wait(dve, stored[p], it * 16)
                nc.vector.tensor_tensor(res[:, p], corr_bank, flat(pooled[:]), ALU.add).then_inc(res_ready, 1)
            pipeline(dve, norm, attend)

        @block.gpsimd
        def _(pool):
            def weigh(tile, p, it):
                pool.wait_ge(z_ready, tile + 1)
                wait(pool, q_ready, tile)
                nc.gpsimd.tensor_tensor(v[:], z[:, p], LA[:], ALU.mult).then_inc(v_ready, 1)
                wait(pool, sc_step, it * 18)
                nc.gpsimd.tensor_tensor(pr[:, p], z[:, p], LG[:], ALU.mult).then_inc(p_ready, 1)
            for p in range(2):
                weigh(p, p, 0)
            with pool.Fori(1, TILES // 2) as it:
                for p in range(2):
                    weigh(it * 2 + p, p, it)

        @block.scalar
        def _(act):
            act.wait_ge(folded, 2)
            nc.scalar.activation(acc[0:D, 3, 0:TN], psum[0:D, BANK:BANK + TN], ACT.Sqrt, scale=1.0 / B, bias=eps[0:D, :]).then_inc(dev_sqrt, 1)

            def deviation(tile, p, it):
                act.wait_ge(m_ready, tile + 1)
                nc.scalar.activation(sq[:], z[:, p], ACT.Square, bias=col[:, p, 1:2], accum_out=col[:, p, 2:3]).then_inc(sq_ready, 1)
                act.wait_ge(sq_ready, tile + 1)
                nc.scalar.activation(col[:, p, 3:4], col[:, p, 2:3], ACT.Sqrt, scale=1.0 / F, bias=eps[:]).then_inc(std_ready, 1)

            def exps(tile, p, it):
                act.wait_ge(shifted, tile + 1)
                nc.scalar.activation(ex[:], sc[:, 0], ACT.Exp).then_inc(exp_ready, 1)
                act.wait_ge(wT_done, tile + 1)
                nc.scalar.copy(wT[:], psum[0:TN, 2 * BANK:2 * BANK + 2 * P].rearrange("p (i b) -> p i b", i=2)).then_inc(wT_ready, 1)
            pipeline(act, deviation, exps)

        @block.tensor
        def _(pe):
            pe.wait_ge(loaded, 16 * N_LOADS)
            pe.wait_ge(st, 4)
            nc.tensor.matmul(psum[:, 0:TN], fold[:], acc[:, 0, 0:TN], start=True, stop=True).then_inc(folded, 1)
            pe.wait_ge(st, ST_VAR)
            nc.tensor.matmul(psum[:, BANK:BANK + TN], fold[:], acc[:, 2, 0:TN], start=True, stop=True).then_inc(folded, 1)

            def correct(tile):
                pe.wait_ge(w_ready, tile + 1)
                wait(pe, wT_ready, tile)
                nc.tensor.transpose(psum[0:TN, 2 * BANK:2 * BANK + P], w[:, 0], ident[:])
                nc.tensor.transpose(psum[0:TN, 2 * BANK + P:2 * BANK + 2 * P], w[:, 1], ident[:]).then_inc(wT_done, 1)
                pe.wait_ge(wT_ready, tile + 1)
                wait(pe, res_ready, tile)
                nc.tensor.matmul(corr_bank, wT[:, 0, :], flat(LBt[:]), start=True, stop=False)
                nc.tensor.matmul(corr_bank, wT[:, 1, :], flat(LGt[:]), start=False, stop=True).then_inc(corr_done, 1)
            correct(0)
            with pe.Fori(1, TILES) as tile:
                correct(tile)


N_LOADS = 8 + 2 * T
ST_VAR = 9
ST_ROWS = 14


def program(nc, ins, out):
    adjT = nc.dram_tensor("adjT", [TILES, N, TN, P], fp32, kind="Internal").ap()
    hB = nc.dram_tensor("hB", [TILES, P, TN, D], fp32, kind="Internal").ap()
    rows_d = nc.dram_tensor("bn_rows_dram", [2, TN, D], fp32, kind="Internal").ap()
    with nc.psum_tensor("psum", [P, 8 * BANK], fp32) as psum:
        stage1(nc, psum, ins["xT"], ins["W"], adjT, ins["ident"])
        with nc.sbuf_tensor("means", [P, TILES, TN], fp32) as means, nc.sbuf_tensor("devs", [P, TILES, TN], fp32) as devs:
            stage2(nc, psum, ins, adjT, hB, (means, devs))
            stage3(nc, psum, ins, hB, rows_d, (means, devs), out)


def kernel(r_x, L0_rec_masker_param, L0_rec_masker_bias, L0_rec_weight, L0_rec_w_ih, L0_rec_w_hh, L0_rec_b_ih, L0_rec_b_hh,
           L0_rec_bn_gamma, L0_rec_bn_beta, L0_rec_ln_gamma, L0_rec_ln_beta, L0_rec_attn_w, L0_rec_attn_b):
    import numpy as np
    import concourse.bacc as bacc
    from concourse.bass_utils import run_bass_kernel_spmd

    x = np.asarray(r_x)
    to = lambda a: np.asarray(a)
    gates = np.stack([to(L0_rec_b_ih).reshape(3, D), to(L0_rec_b_hh).reshape(3, D)]).transpose(2, 0, 1)
    arrays = {
        "xT": np.concatenate([x.reshape(B, KX).T, np.ones((1, B), x.dtype)]),
        "W": np.concatenate([to(L0_rec_masker_param).transpose(1, 0, 2).reshape(KX, T * N * N),
                             to(L0_rec_masker_bias).reshape(1, T * N * N)]),
        "ident": np.eye(P, dtype=x.dtype),
        "fold": np.tile(np.eye(D, dtype=x.dtype), (4, 4)),
        "xm": x.transpose(1, 0, 2),
        "xg": x.reshape(TILES, 4, 32, N, D).transpose(0, 1, 4, 2, 3).reshape(TILES, P, 32, N),
        "wT4": np.tile(to(L0_rec_weight)[0].T, (1, 4)),
        "wihT": to(L0_rec_w_ih).T,
        "whhT4": np.tile(to(L0_rec_w_hh).T, (4, 1)),
        "biases": np.tile(gates, (4, 1, 1)),
        "bn_gamma": to(L0_rec_bn_gamma).reshape(TN, D).T,
        "bn_beta": to(L0_rec_bn_beta).reshape(TN, D).T,
        "ln_gamma": to(L0_rec_ln_gamma).reshape(TN, D),
        "ln_beta": to(L0_rec_ln_beta).reshape(TN, D),
        "attn_w": to(L0_rec_attn_w).reshape(D),
        "attn_b": to(L0_rec_attn_b).reshape(1),
    }
    arrays = {name: np.ascontiguousarray(a) for name, a in arrays.items()}
    nc = bacc.Bacc("TRN2", target_bir_lowering=False, num_devices=1)
    ins = {name: nc.dram_tensor(name, a.shape, mybir.dt.from_np(a.dtype), kind="ExternalInput").ap() for name, a in arrays.items()}
    out = nc.dram_tensor("out", [TILES, P, T * D], fp32, kind="ExternalOutput").ap()
    program(nc, ins, out)
    result = run_bass_kernel_spmd(nc, [arrays], core_ids=[0])
    return result.results[0]["out"].reshape(B, T * D)
```

```python
import concourse.bass as bass
from concourse import mybir
from contextlib import ExitStack

fp32 = mybir.dt.float32
fp32r = mybir.dt.float32r
ALU = mybir.AluOpType
ACT = mybir.ActivationFunctionType
AX = mybir.AxisListType

B, N, D, T = 2048, 50, 32, 2
TN = T * N
P = 128
TILES = B // P
KX = N * D
KROWS = KX + 1
KC = (KROWS + P - 1) // P
KLAST = KROWS - (KC - 1) * P
GN = 10
GW = GN * N
GROUPS = T * N // GN
BLK = 8
BLOCKS = TILES // BLK
ITERS = BLOCKS * GROUPS
MPAD = 64
PAIRS = GN // 2
EPS_ROW = 1e-6
EPS = 1e-5
UNITS = [(u, min(u + 2, KC)) for u in range(0, KC, 2)]
NU = len(UNITS)
T_AT = 3

BANK = 512

QB = 4
ROUNDS = 32 // QB
RC = QB * TN
XPARTS = 4
XG = 32 // XPARTS
TPARTS = 4
TC = TN // TPARTS
R_G, Z_G, N_G = 0, 1, 2
FQ = P // D
FC = TN // FQ
F = TN * D
CB = 4
CW = CB * P
QC = (FC + 3) // 4
QR = FQ * QC
PIECES = 5


def wait(eng, sem, value):
    if not (isinstance(value, int) and value <= 0):
        eng.wait_ge(sem, value)


def stage1(nc, psum, xT, W, adjT, ident_d):
    with ExitStack() as ctx:
        sb = lambda name, shape, dt=fp32: ctx.enter_context(nc.sbuf_tensor(name, shape, dt))
        sem = lambda name: ctx.enter_context(nc.semaphore(name))
        x_hi = sb("x_hi", [P, KC, BLK * P], fp32r)
        x_lo = sb("x_lo", [P, KC, BLK * P], fp32r)
        x_raw = sb("x_raw", [P, KC, P])
        w_hi = sb("w_hi", [P, KC, GW], fp32r)
        w_lo = sb("w_lo", [P, KC, GW], fp32r)
        w_raw = sb("w_raw", [P, KC, GW])
        ident = sb("ident_sb", [P, P])
        u = sb("u", [P, 2, GN, N])
        an = sb("an", [P, 2, PAIRS, 2, MPAD])
        rows = sb("rows", [P, 3, GN])
        at = sb("at", [P, 2, PAIRS, P])

        x_loaded, ident_loaded = sem("x_loaded"), sem("ident_loaded")
        w_loaded = [sem(f"w_loaded{i}") for i in range(NU)]
        x_hi_ready, x_ready = sem("x_hi_ready"), sem("x_ready")
        w_hi_ready, w_ready, w_used = sem("w_hi_ready"), sem("w_ready"), sem("w_used")
        mm_done, u_ready, an_ready = sem("mm_done"), sem("u_ready"), sem("an_ready")
        tr_done, at_ready = sem("tr_done"), sem("at_ready")
        at_stored = [sem("at_stored0"), sem("at_stored1")]
        pad_zeroed, dve_step = sem("pad_zeroed"), sem("dve_step")

        def mm_out(c2):
            return psum[:, c2 * BANK:c2 * BANK + GW]

        def tr_out(c2):
            return psum[:, (2 + 2 * c2) * BANK:(2 + 2 * c2) * BANK + PAIRS * P]

        xT_main = xT[0:(KC - 1) * P, :].rearrange("(k p) b -> p k b", p=P)
        W_main = W[0:(KC - 1) * P, :].rearrange("(k p) n -> p k n", p=P)
        block = ctx.enter_context(nc.Block())

        @block.sync
        def _(sp):
            def load_x(bt):
                if bt >= 1:
                    sp.wait_ge(x_ready, bt)
                sp.dma_start(x_raw[:, 0:KC - 1, :], xT_main[:, :, bt * P:(bt + 1) * P]).then_inc(x_loaded, 16)
                sp.dma_start(x_raw[0:KLAST, KC - 1, :],
                             xT[(KC - 1) * P:KROWS, bt * P:(bt + 1) * P]).then_inc(x_loaded, 16)

            def load_w(i, group, after):
                k0, k1 = UNITS[i]
                if after is not None:
                    sp.wait_ge(w_ready, after)
                cols = bass.ds(group * GW, GW)
                if k1 < KC:
                    sp.dma_start(w_raw[:, k0:k1, :], W_main[:, k0:k1, cols]).then_inc(w_loaded[i], 16)
                else:
                    sp.dma_start(w_raw[0:KLAST, k0, :], W[(KC - 1) * P:KROWS, cols]).then_inc(w_loaded[i], 16)

            def store_tile(c, c2, tile, group):
                sp.wait_ge(at_ready, c + 1)
                for half in range(2):
                    sp.dma_start(adjT[tile, :, bass.ds(group * GN + half * PAIRS, PAIRS), :],
                                 at[MPAD * half:MPAD * half + N, c2, :, :]).then_inc(at_stored[c2], 16)

            load_x(0)
            for i in range(NU):
                load_w(i, 0, None)
            sp.dma_start(ident[:, :], ident_d).then_inc(ident_loaded, 16)
            for blk in range(BLOCKS):
                for it, group in p1_iters(sp, blk):
                    for w in range(BLK):
                        if isinstance(it, int) and it == 0 and w + 1 < BLK:
                            load_x(w + 1)
                        if w == 1 and not (isinstance(it, int) and it == ITERS - 1):
                            nxt = 0 if isinstance(it, int) and it % GROUPS == GROUPS - 1 else group + 1
                            for i in range(NU):
                                load_w(i, nxt, it * NU + i + 1)
                        c = it * BLK + w
                        if w > 0:
                            store_tile(c - 1, (w - 1) % 2, blk * BLK + w - 1, group)
                        elif not (isinstance(it, int) and it == 0):
                            if isinstance(it, int) and it % GROUPS == 0:
                                store_tile(c - 1, 1, blk * BLK - 1, GROUPS - 1)
                            else:
                                store_tile(c - 1, 1, blk * BLK + BLK - 1, group - 1)
                        if isinstance(it, int) and it == GROUPS - 1 and blk + 1 < BLOCKS and w >= 1:
                            load_x(BLK + w - 1)
                    if isinstance(it, int) and it == GROUPS - 1 and blk + 1 < BLOCKS:
                        load_x(2 * BLK - 1)
            store_tile(ITERS * BLK - 1, 1, TILES - 1, GROUPS - 1)
            sp.wait_ge(at_stored[0], 32 * (ITERS * BLK // 2))
            sp.wait_ge(at_stored[1], 32 * (ITERS * BLK // 2))

        def split_x_hi(act, bt):
            act.wait_ge(x_loaded, 32 * (bt + 1))
            if bt >= BLK:
                act.wait_ge(mm_done, (GROUPS - 1) * BLK + bt - BLK + 1)
            cols = bass.ts(bt % BLK, P)
            nc.scalar.copy(x_hi[:, 0:KC - 1, cols], x_raw[:, 0:KC - 1, :])
            nc.scalar.copy(x_hi[0:KLAST, KC - 1, cols], x_raw[0:KLAST, KC - 1, :]).then_inc(x_hi_ready, 1)

        def split_x_lo(dve, bt):
            dve.wait_ge(x_hi_ready, bt + 1)
            cols = bass.ts(bt % BLK, P)
            for rows_, ks in ((P, slice(0, KC - 1)), (KLAST, slice(KC - 1, KC))):
                last = nc.vector.tensor_tensor(x_lo[0:rows_, ks, cols], x_raw[0:rows_, ks, :],
                                               x_hi[0:rows_, ks, cols].bitcast(fp32), ALU.subtract)
            last.then_inc(x_ready, 1)

        def split_w_hi(act, i, it):
            act.wait_ge(w_loaded[i], (it + 1) * 16)
            if not (isinstance(it, int) and it == 0):
                if i == NU - 1:
                    act.wait_ge(mm_done, it * BLK)
                else:
                    act.wait_ge(w_used, (it - 1) * (NU - 1) + i + 1)
            k0, k1 = UNITS[i]
            r = P if k1 < KC else KLAST
            nc.scalar.copy(w_hi[0:r, k0:k1, :], w_raw[0:r, k0:k1, :]).then_inc(w_hi_ready, 1)

        def split_w_lo(dve, i, it):
            dve.wait_ge(w_hi_ready, it * NU + i + 1)
            k0, k1 = UNITS[i]
            r = P if k1 < KC else KLAST
            nc.vector.tensor_tensor(w_lo[0:r, k0:k1, :], w_raw[0:r, k0:k1, :],
                                    w_hi[0:r, k0:k1, :].bitcast(fp32), ALU.subtract).then_inc(w_ready, 1)

        @block.scalar
        def _(act):
            def relu(c, c2, start=False):
                act.wait_ge(mm_done, c + 1)
                if not start:
                    act.wait_ge(an_ready, c - 1)
                nc.scalar.activation(u[:, c2].rearrange("p n m -> p (n m)"), mm_out(c2), ACT.Relu).then_inc(u_ready, 1)

            def evacuate(c, c2, start=False):
                act.wait_ge(tr_done, c + 1)
                if not start:
                    act.wait_ge(at_stored[c2], 16 * (c - c2))
                nc.scalar.copy(at[:, c2].rearrange("p q b -> p (q b)"), tr_out(c2)).then_inc(at_ready, 1)

            split_x_hi(act, 0)
            for i in range(NU):
                split_w_hi(act, i, 0)
            for blk in range(BLOCKS):
                for it, group in p1_iters(act, blk):
                    static = isinstance(it, int)
                    for w in range(BLK):
                        c = it * BLK + w
                        split = w == BLK - 1 and not (static and it == ITERS - 1)
                        if not (static and it == 0 and w == 0):
                            relu(c - 1, (w - 1) % 2, start=static and it == 0 and w <= 2)
                        if static and it == 0 and w + 1 < BLK:
                            split_x_hi(act, w + 1)
                        if split:
                            for i in range(0, T_AT + 1):
                                split_w_hi(act, i, it + 1)
                        if not (static and it == 0 and w == 0):
                            evacuate(c - 1, (w - 1) % 2, start=static and it == 0 and w <= 2)
                        if split:
                            for i in range(T_AT + 1, NU):
                                split_w_hi(act, i, it + 1)
                        if static and it == GROUPS - 1 and w >= 1:
                            split_x_hi(act, BLK + w - 1)
                    if static and it == GROUPS - 1:
                        split_x_hi(act, 2 * BLK - 1)
            c = ITERS * BLK - 1
            relu(c, 1)
            evacuate(c, 1)

        @block.vector
        def _(dve):
            nc.vector.memset(an[:].rearrange("p c q h m -> p (c q h m)"), 0.0).then_inc(pad_zeroed, 1)
            dve.wait_ge(pad_zeroed, 1)

            def normalise(c, c2, start=False):
                dve.wait_ge(u_ready, c + 1)
                nc.vector.tensor_reduce(rows[:, 0], u[:, c2], AX.X, ALU.add).then_inc(dve_step, 1)
                dve.wait_ge(dve_step, 3 * c + 1)
                nc.vector.tensor_scalar_add(rows[:, 1], rows[:, 0], EPS_ROW).then_inc(dve_step, 1)
                dve.wait_ge(dve_step, 3 * c + 2)
                nc.vector.reciprocal(rows[:, 2], rows[:, 1]).then_inc(dve_step, 1)
                dve.wait_ge(dve_step, 3 * c + 3)
                if not start:
                    dve.wait_ge(tr_done, c - 1)
                nc.vector.tensor_tensor(an[:, c2, :, :, 0:N].rearrange("p q h m -> p h q m"),
                                        u[:, c2].rearrange("p (h q) m -> p h q m", h=2),
                                        rows[:, 2].rearrange("p (h q) -> p h q", h=2).unsqueeze(3).to_broadcast([P, 2, PAIRS, N]),
                                        ALU.mult).then_inc(an_ready, 1)

            split_x_lo(dve, 0)
            for i in range(NU):
                split_w_lo(dve, i, 0)
            for blk in range(BLOCKS):
                for it, group in p1_iters(dve, blk):
                    static = isinstance(it, int)
                    for w in range(BLK):
                        c = it * BLK + w
                        if not (static and it == 0 and w == 0):
                            normalise(c - 1, (w - 1) % 2, start=static and it == 0 and w <= 2)
                        if static and it == 0 and w + 1 < BLK:
                            split_x_lo(dve, w + 1)
                        if w == BLK - 1 and not (static and it == ITERS - 1):
                            for i in range(NU):
                                split_w_lo(dve, i, it + 1)
                        if static and it == GROUPS - 1 and w >= 1:
                            split_x_lo(dve, BLK + w - 1)
                    if static and it == GROUPS - 1:
                        split_x_lo(dve, 2 * BLK - 1)
            normalise(ITERS * BLK - 1, 1)

        @block.tensor
        def _(pe):
            def transposes(c, c2, start=False):
                pe.wait_ge(an_ready, c + 1)
                if not start:
                    pe.wait_ge(at_ready, c - 1)
                for q in range(PAIRS):
                    last = nc.tensor.transpose(tr_out(c2)[:, q * P:(q + 1) * P],
                                               an[:, c2, q].rearrange("p h m -> p (h m)"), ident[:, :])
                last.then_inc(tr_done, 1)

            def window(it, w, blk, c, start=False, bank_free=False, none_before=False):
                pe.wait_ge(x_ready, blk * BLK + w + 1)
                if not bank_free:
                    pe.wait_ge(u_ready, c - 1)
                cols = bass.ts(w, P)
                for i, (k0, k1) in enumerate(UNITS):
                    if w == 0:
                        pe.wait_ge(w_ready, it * NU + i + 1)
                    for k in range(k0, k1):
                        r = P if k < KC - 1 else KLAST
                        for n, (a, b) in enumerate(((x_lo, w_hi), (x_hi, w_lo), (x_hi, w_hi))):
                            last = nc.tensor.matmul(mm_out(w % 2), a[0:r, k, cols], b[0:r, k, :],
                                                    start=(k == 0 and n == 0), stop=(k == KC - 1 and n == 2))
                    if i == NU - 1:
                        last.then_inc(mm_done, 1)
                    elif w == BLK - 1:
                        last.then_inc(w_used, 1)
                    if i == T_AT and not none_before:
                        transposes(c - 1, (w - 1) % 2, start=start)

            pe.wait_ge(ident_loaded, 16)
            for blk in range(BLOCKS):
                for it, group in pe_iters(pe, blk):
                    static = isinstance(it, int)
                    for w in range(BLK):
                        c = it * BLK + w
                        window(it, w, blk, c, start=static and it == 0 and w <= 2,
                               bank_free=static and it == 0 and w < 2, none_before=static and it == 0 and w == 0)
            transposes(ITERS * BLK - 1, 1)


def p1_iters(eng, blk):
    base = blk * GROUPS
    yield base, 0
    with eng.Fori(1, GROUPS - 1) as g:
        yield base + g, g
    yield base + GROUPS - 1, GROUPS - 1


def pe_iters(eng, blk):
    base = blk * GROUPS
    if blk == 0:
        yield 0, 0
    with eng.Fori(1 if blk == 0 else 0, GROUPS) as g:
        yield base + g, g


def stage2(nc, psum, ins, adjT, hF, stats):
    with ExitStack() as ctx:
        sb = lambda name, shape, dt=fp32: ctx.enter_context(nc.sbuf_tensor(name, shape, dt))
        sem = lambda name: ctx.enter_context(nc.semaphore(name))
        adj = sb("adj_sb", [P, TN, P])
        xs = sb("xs_sb", [P, P, D])
        xg = sb("xg_sb", [P, 2, 32, N])
        xg_hi = sb("xg_hi", [P, 2, 32, N], fp32r)
        xg_lo = sb("xg_lo", [P, 2, 32, N], fp32r)
        hG = sb("hG", [P, 2, 32, TN])
        hT = sb("hT", [P, TN, D])
        hC = sb("hC", [P, FC, P])
        ident = sb("ident2_sb", [P, P])
        m_hi = sb("m_hi", [P, 2, RC], fp32r)
        m_lo = sb("m_lo", [P, 2, RC], fp32r)
        r_gate = sb("r_gate", [P, 2, RC])
        z_gate = sb("z_gate", [P, 2, RC])
        n_in = sb("n_in", [P, 2, RC])
        n_gate = sb("n_gate", [P, 2, RC])
        part = sb("part", [P, 8, TN])
        share = sb("share", [P, 1])
        wT4 = sb("wT4_sb", [D, P])
        wih = sb("wih_sb", [D, 3 * D])
        whh4 = sb("whh_sb", [P, 3 * D])
        biases = sb("biases_sb", [P, 2, 3])
        bias = sb("bias", [P, 3])
        wd = sb("wd", [P, 2, 3, P])
        wd_hi = sb("wd_hi", [P, 2, 3, P], fp32r)
        wd_lo = sb("wd_lo", [P, 2, 3, P], fp32r)
        means, devs = stats

        consts_loaded, ident_loaded = sem("consts_loaded"), sem("ident_loaded")
        g_product, zeroed, blocks_ready = sem("g_product"), sem("zeroed"), sem("blocks_ready")
        wd_hi_ready, wd_ready, bias_ready = sem("wd_hi_ready"), sem("wd_ready"), sem("bias_ready")
        adj_loaded = [sem("adj_loaded0"), sem("adj_loaded1")]
        xg_loaded = [sem("xg_loaded0"), sem("xg_loaded1")]
        xg_hi_ready, xg_ready = sem("xg_hi_ready"), sem("xg_ready")
        ax_done, m_hi_ready, m_ready = sem("ax_done"), sem("m_hi_ready"), sem("m_ready")
        gate_done = [sem(f"{g}_done") for g in ("r", "z", "n")]
        r_ready, z_ready, n_in_ready, n_ready = sem("r_ready"), sem("z_ready"), sem("n_in_ready"), sem("n_ready")
        d_step, h_ready = sem("d_step"), sem("h_ready")
        hT_ready = sem("hT_ready")
        turned, hC_ready, hC_stored = sem("turned"), sem("hC_ready"), sem("hC_stored")
        pool_step, share_ready = sem("pool_step"), sem("share_ready")
        hG_free = [sem("hG_free0"), sem("hG_free1")]

        S = 2 * ROUNDS
        ax_bank = lambda s: psum[:, (s % 2) * BANK:(s % 2) * BANK + RC]

        def gate_bank(gate, s):
            bank = {R_G: 2 + s % 2, N_G: 4 + s % 2, Z_G: 6}[gate]
            return psum[:, bank * BANK:bank * BANK + RC]

        turn_bank = psum[:, 7 * BANK:8 * BANK]
        batches = [(c, min(c + 4, FC)) for c in range(0, FC, 4)]
        assert len(batches) == ROUNDS - 1
        block = ctx.enter_context(nc.Block())

        @block.sync
        def _(sp):
            def load_adj(tile, r):
                sp.dma_start(adj[MPAD * r:MPAD * r + N, :, :], adjT[tile]).then_inc(adj_loaded[r], 16)
                sp.dma_start(xs[MPAD * r:MPAD * r + N, :, :],
                             ins["xm"][:, bass.ds(tile * P, P), :]).then_inc(adj_loaded[r], 16)

            def load_xg(tile, r):
                sp.dma_start(xg[:, r], ins["xg"][tile]).then_inc(xg_loaded[r], 16)

            def iteration(it, more):
                for r in range(2):
                    tile = it * 2 + r
                    if more:
                        sp.wait_ge(ax_done, (tile + 1) * ROUNDS)
                        load_adj(tile + 2, r)
                    if r or not (isinstance(it, int) and it == 0):
                        store(tile - 1)
                    sp.wait_ge(h_ready, (tile + 1) * ROUNDS)
                    if more:
                        load_xg(tile + 2, r)

            def store(tile):
                sp.wait_ge(hC_ready, (tile + 1) * len(batches))
                sp.dma_start(hF[tile], hC[:]).then_inc(hC_stored, 16)

            for dst, src in ((wT4, "wT4"), (wih, "wihT"), (whh4, "whhT4"), (biases, "biases")):
                sp.dma_start(dst[:], ins[src]).then_inc(consts_loaded, 16)
            load_xg(0, 0)
            load_adj(0, 0)
            sp.dma_start(ident[:], ins["ident"]).then_inc(ident_loaded, 16)
            load_xg(1, 1)
            load_adj(1, 1)
            iteration(0, True)
            with sp.Fori(1, TILES // 2 - 1) as it:
                iteration(it, True)
            iteration(TILES // 2 - 1, False)
            store(TILES - 1)
            sp.wait_ge(hC_stored, 16 * TILES)

        @block.scalar
        def _(act):
            act.wait_ge(blocks_ready, 1)
            nc.scalar.copy(wd_hi[:], wd[:]).then_inc(wd_hi_ready, 1)
            act.wait_ge(bias_ready, 1)

            def x_hi(it, r, k):
                if k == 0:
                    act.wait_ge(xg_loaded[r], (it + 1) * 16)
                    wait(act, gate_done[Z_G], it * S if r else it * S - ROUNDS)
                g = slice(k * XG, (k + 1) * XG)
                nc.scalar.copy(xg_hi[:, r, g], xg[:, r, g]).then_inc(xg_hi_ready, 1)

            def m_halves(it, s):
                act.wait_ge(ax_done, it * S + s + 1)
                nc.scalar.copy(m_hi[:, s % 2], ax_bank(s)).then_inc(m_hi_ready, 1)

            def evacuate(tile, n):
                act.wait_ge(turned, tile * len(batches) + n + 1)
                if n == 0:
                    wait(act, hC_stored, 16 * tile)
                c0, c1 = batches[n]
                nc.scalar.copy(hC[:, c0:c1, :].rearrange("p c b -> p (c b)"),
                               turn_bank[:, 0:(c1 - c0) * P]).then_inc(hC_ready, 1)

            def turn(it, more):
                for s in range(S):
                    r, q = divmod(s, ROUNDS)
                    if q and (r or not (isinstance(it, int) and it == 0)):
                        evacuate(it * 2 + r - 1, q - 1)
                    if s + 1 < S or more:
                        wait(act, gate_done[Z_G], it * S + s)
                        m_halves(it + (s + 1) // S, (s + 1) % S)
                    k = s % ROUNDS - (ROUNDS - 1 - XPARTS)
                    if 0 <= k < XPARTS and (s < ROUNDS or more):
                        x_hi(it + s // ROUNDS, 1 - s // ROUNDS, k)
                    act.wait_ge(gate_done[R_G], it * S + s + 1)
                    wait(act, h_ready, it * S + s - 1)
                    nc.scalar.activation(r_gate[:, s % 2], gate_bank(R_G, s), ACT.Sigmoid,
                                         bias=bias[:, R_G:R_G + 1]).then_inc(r_ready, 1)
                    act.wait_ge(gate_done[Z_G], it * S + s + 1)
                    nc.scalar.activation(z_gate[:, s % 2], gate_bank(Z_G, s), ACT.Sigmoid,
                                         bias=bias[:, Z_G:Z_G + 1]).then_inc(z_ready, 1)
                    act.wait_ge(n_in_ready, it * S + s + 1)
                    nc.scalar.activation(n_gate[:, s % 2], n_in[:, s % 2], ACT.Tanh).then_inc(n_ready, 1)

            for k in range(XPARTS):
                x_hi(0, 0, k)
            m_halves(0, 0)
            turn(0, True)
            with act.Fori(1, TILES // 2 - 1) as it:
                turn(it, True)
            turn(TILES // 2 - 1, False)
            for n in range(len(batches)):
                evacuate(TILES - 1, n)

        @block.vector
        def _(dve):
            nc.vector.memset(wd[:], 0.0).then_inc(zeroed, 1)
            dve.wait_ge(zeroed, 1)
            dve.wait_ge(consts_loaded, 64)
            dve.wait_ge(g_product, 1)
            for j in range(4):
                q = slice(D * j, D * j + D)
                nc.vector.tensor_copy(wd[q, 0, :, q], psum[q, 0:3 * D].rearrange("p (g e) -> p g e", g=3))
                last = nc.vector.tensor_copy(wd[q, 1, :, q], whh4[q, :].rearrange("p (g e) -> p g e", g=3))
            last.then_inc(blocks_ready, 1)
            nc.vector.tensor_tensor(bias[:], biases[:, 0], biases[:, 1], ALU.add).then_inc(bias_ready, 1)
            dve.wait_ge(wd_hi_ready, 1)
            nc.vector.tensor_tensor(wd_lo[:], wd[:], wd_hi[:].bitcast(fp32), ALU.subtract).then_inc(wd_ready, 1)
            dve.wait_ge(bias_ready, 1)
            def x_lo(it, r, k):
                dve.wait_ge(xg_hi_ready, (it * 2 + r) * XPARTS + k + 1)
                g = slice(k * XG, (k + 1) * XG)
                nc.vector.tensor_tensor(xg_lo[:, r, g], xg[:, r, g], xg_hi[:, r, g].bitcast(fp32),
                                        ALU.subtract).then_inc(xg_ready, 1)

            def m_halves(it, s):
                dve.wait_ge(m_hi_ready, it * S + s + 1)
                nc.vector.tensor_tensor(m_lo[:, s % 2], ax_bank(s), m_hi[:, s % 2].bitcast(fp32),
                                        ALU.subtract).then_inc(m_ready, 1)

            def nodes(ap):
                return ap.rearrange("p (g t n) -> p g t n", g=QB, t=T)

            def update(it, s):
                dve.wait_ge(gate_done[N_G], it * S + s + 1)
                dve.wait_ge(r_ready, it * S + s + 1)
                nc.vector.scalar_tensor_tensor(out=n_in[:, s % 2], in0=gate_bank(N_G, s), scalar=bias[:, N_G:N_G + 1],
                                               in1=r_gate[:, s % 2], op0=ALU.add, op1=ALU.mult).then_inc(n_in_ready, 1)

            def finish(it, s):
                r, q = divmod(s, ROUNDS)
                base = (it * S + s) * 2
                dve.wait_ge(n_ready, it * S + s + 1)
                diff = n_in[:, s % 2]
                x_b = xg[:, r, q * QB:(q + 1) * QB, :].unsqueeze(2).to_broadcast([P, QB, T, N])
                nc.vector.tensor_tensor(nodes(diff), x_b, nodes(n_gate[:, s % 2]), ALU.subtract).then_inc(d_step, 1)
                dve.wait_ge(d_step, base + 1)
                dve.wait_ge(z_ready, it * S + s + 1)
                nc.vector.tensor_tensor(diff, diff, z_gate[:, s % 2], ALU.mult).then_inc(d_step, 1)
                dve.wait_ge(d_step, base + 2)
                nc.vector.tensor_tensor(hG[:, r, q * QB:(q + 1) * QB, :].rearrange("p g c -> p (g c)"), diff,
                                        n_gate[:, s % 2], ALU.add).then_inc(h_ready, 1)

            def turn_rows(it, r, k):
                tile = it * 2 + r
                if k == 0:
                    dve.wait_ge(h_ready, (tile + 1) * ROUNDS)
                    wait(dve, turned, tile * len(batches))
                c = slice(k * TC, (k + 1) * TC)
                nc.vector.transpose(hT[:, c], hG[:, r, :, c].rearrange("p g c -> p c g")).then_inc(hT_ready, 1)

            def turn(it, more):
                for s in range(S):
                    if s + 1 < S or more:
                        m_halves(it + (s + 1) // S, (s + 1) % S)
                    k = s % ROUNDS - (ROUNDS - 1 - XPARTS)
                    if 0 <= k < XPARTS and (s < ROUNDS or more):
                        x_lo(it + s // ROUNDS, 1 - s // ROUNDS, k)
                    update(it, s)
                    if s % ROUNDS == 0:
                        wait(dve, hG_free[s // ROUNDS], it)
                    finish(it, s)
                    r, q = divmod(s, ROUNDS)
                    if q == ROUNDS - 1:
                        turn_rows(it, r, 0)
                    elif q < TPARTS - 1 and r:
                        turn_rows(it, 0, q + 1)
                    elif q < TPARTS - 1 and not (isinstance(it, int) and it == 0):
                        turn_rows(it - 1, 1, q + 1)

            for k in range(XPARTS):
                x_lo(0, 0, k)
            m_halves(0, 0)
            turn(0, True)
            with dve.Fori(1, TILES // 2 - 1) as it:
                turn(it, True)
            turn(TILES // 2 - 1, False)
            for k in range(1, TPARTS):
                turn_rows(TILES // 2 - 1, 1, k)

        @block.gpsimd
        def _(pool):
            TT = nc.gpsimd.tensor_tensor
            nc.gpsimd.memset(share[:], 1.0 / 32).then_inc(share_ready, 1)
            pool.wait_ge(share_ready, 1)
            with pool.Fori(0, TILES // 2) as it:
                for r in range(2):
                    tile = it * 2 + r
                    step = [tile * 14]

                    def chain(ins_):
                        step[0] = step[0] + 1
                        ins_.then_inc(pool_step, 1)
                        pool.wait_ge(pool_step, step[0])

                    h = hG[:, r]
                    mean = part[:, 1:2]
                    pool.wait_ge(h_ready, (tile + 1) * ROUNDS)
                    chain(TT(part[:], h[:, 0:8], h[:, 8:16], ALU.add))
                    chain(TT(part[:], part[:], h[:, 16:24], ALU.add))
                    chain(TT(part[:], part[:], h[:, 24:32], ALU.add))
                    for g in (4, 2, 1):
                        chain(TT(part[:, 0:g], part[:, 0:g], part[:, g:2 * g], ALU.add))
                    for to in (mean, means[:, bass.ds(tile, 1), :]):
                        chain(TT(to, part[:, 0:1], share[:].unsqueeze(1).to_broadcast([P, 1, TN]), ALU.mult))
                    pool.wait_ge(hT_ready, (tile + 1) * TPARTS)
                    chain(TT(h, h, mean.to_broadcast([P, 32, TN]), ALU.subtract))
                    chain(TT(h, h, h, ALU.mult))
                    for g in (16, 8, 4, 2):
                        chain(TT(h[:, 0:g], h[:, 0:g], h[:, g:2 * g], ALU.add))
                    TT(devs[:, bass.ds(tile, 1), :], h[:, 0:1], h[:, 1:2], ALU.add).then_inc(hG_free[r], 1)
                    pool.wait_ge(hG_free[r], it + 1)

        @block.tensor
        def _(pe):
            pe.wait_ge(consts_loaded, 64)
            nc.tensor.matmul(psum[:, 0:3 * D], wT4[:], wih[:], start=True, stop=True).then_inc(g_product, 1)
            pe.wait_ge(wd_ready, 1)

            def aggregate(s):
                r, q = divmod(s, ROUNDS)
                rows = slice(MPAD * r, MPAD * r + N)
                for gi in range(QB):
                    for j in range(4):
                        b = 32 * j + q * QB + gi
                        last = nc.tensor.matmul(ax_bank(s)[D * j:D * j + D, gi * TN:(gi + 1) * TN],
                                                xs[rows, b, :], adj[rows, :, b], start=True, stop=True)
                last.then_inc(ax_done, 1)

            def gates(it, s, more):
                r, q = divmod(s, ROUNDS)
                if q == 0:
                    pe.wait_ge(xg_ready, (it * 2 + r + 1) * XPARTS)
                if s == ROUNDS - 2:
                    pe.wait_ge(adj_loaded[1], (it + 1) * 32)
                if s == S - 2 and more:
                    pe.wait_ge(adj_loaded[0], (it + 2) * 32)
                pe.wait_ge(m_ready, it * S + s + 1)
                xb = [t[:, r, q * QB:(q + 1) * QB, :].unsqueeze(2).to_broadcast([P, QB, T, N]) for t in (xg_hi, xg_lo)]
                for gate in (R_G, N_G, Z_G):
                    if gate == Z_G:
                        if q and (r or not (isinstance(it, int) and it == 0)):
                            turn_chunks(it * 2 + r - 1, q - 1)
                        wait(pe, z_ready, it * S + s)
                    else:
                        wait(pe, n_in_ready if gate == N_G else r_ready, it * S + s - 1)
                    terms = []
                    for part, (hi, lo) in enumerate(((m_hi[:, s % 2], m_lo[:, s % 2]), xb)):
                        terms += [(wd_lo[:, part, gate], hi), (wd_hi[:, part, gate], lo), (wd_hi[:, part, gate], hi)]
                    for i, (w, m) in enumerate(terms):
                        last = nc.tensor.matmul(gate_bank(gate, s), w, m, start=i == 0, stop=i == len(terms) - 1)
                    last.then_inc(gate_done[gate], 1)

            def turn_chunks(tile, n):
                c0, c1 = batches[n]
                pe.wait_ge(hT_ready, tile * TPARTS + (c1 * FQ + TC - 1) // TC)
                wait(pe, hC_ready, tile * len(batches) + n)
                features = hT[:].rearrange("p c d -> p (c d)")
                for c in range(c0, c1):
                    last = nc.tensor.transpose(turn_bank[:, (c - c0) * P:(c - c0 + 1) * P],
                                               features[:, c * P:(c + 1) * P], ident[:])
                last.then_inc(turned, 1)

            def turn(it, more):
                for s in range(S):
                    if s + 1 < S or more:
                        aggregate((s + 1) % S)
                    gates(it, s, more)

            pe.wait_ge(adj_loaded[0], 32)
            aggregate(0)
            pe.wait_ge(ident_loaded, 16)
            turn(0, True)
            with pe.Fori(1, TILES // 2 - 1) as it:
                turn(it, True)
            turn(TILES // 2 - 1, False)
            for n in range(len(batches)):
                turn_chunks(TILES - 1, n)


def stage3(nc, psum, ins, hF, stats, out):
    with ExitStack() as ctx:
        sb = lambda name, shape, dt=fp32: ctx.enter_context(nc.sbuf_tensor(name, shape, dt))
        sem = lambda name: ctx.enter_context(nc.semaphore(name))
        means, devs = stats
        SW = 4 * QR
        ident = sb("ident3_sb", [P, P])
        fold = sb("fold_sb", [P, P])
        quarter = sb("quarter_sb", [P, FQ, P])
        ones = sb("ones_sb", [P, P])
        score_mask = sb("score_mask_sb", [P, FC, D])
        sum_mask = sb("sum_mask_sb", [P, D])
        square_mask = sb("square_mask_sb", [P, D])
        pool_mask = sb("pool_mask_sb", [P, FC + 1, D])
        spread = sb("spread_sb", [TN, FC, P], fp32r)
        fold_out = sb("fold_out_sb", [P, T * D])
        par = sb("par_sb", [P, 4, FC])
        aw = sb("awF_sb", [P, 1])
        ab = sb("abF_sb", [P, 1])
        rowpar = sb("rowpar_sb", [TN, 3, D])
        t_mask = sb("t_mask_sb", [TN, T])
        rowblk = sb("rowblk", [TN, 3, T, D])
        eps = sb("eps3", [P, 1])
        fsum = sb("fsum", [P, 2, TN])
        mean_rep = sb("mean_rep", [P, TN])
        mdev = sb("mdev", [P, TILES, TN])
        mu, var, std, inv = (sb(n, [P, FC]) for n in ("mu_sb", "var_sb", "bnstd_sb", "inv_sb"))
        nmu, A, Amu, C, Csq = (sb(n, [P, FC]) for n in ("nmu_sb", "A_sb", "Amu_sb", "C_sb", "Csq_sb"))
        LA, ALA, CLA, LBA, ALG = (sb(n, [P, FC]) for n in ("LA_sb", "ALA_sb", "CLA_sb", "LBA_sb", "ALG_sb"))
        sums = sb("sums_sb", [P, 2])
        c0 = sb("c0_sb", [P, 1])
        csum = sb("csum_sb", [P, 1])
        score_cols = sb("score_cols", [P, FC, D])
        sum_cols = sb("sum_cols", [P, FC, D])
        pool_cols = sb("pool_cols", [P, FC + 1, D])
        K = sb("K_sb", [P, 3, SW])
        h = sb("h3", [P, 2, FC, CW])
        spread_raw = h[0:TN, 1].rearrange("p c b -> p (c b)")[:, 0:FC * P]
        sq = sb("sq3", [P, 4, CW])
        pr = sb("pr3", [P, 3, CW])
        qs = sb("qs", [P, CW])
        st = sb("row_stats", [P, 9, CB])
        sc = sb("sc3", [P, 3, CB, SW])
        mx = sb("mx3", [P, 3, CB, T])
        w = sb("w3", [P, 3, CB, TN])
        wT = sb("wT3", [TN, 3, CW])
        w_hi = sb("w_hi3", [TN, CW], fp32r)
        w_lo = sb("w_lo3", [TN, CW], fp32r)
        O_sb = sb("O_sb", [P, CW])
        res = sb("res3", [T * D, 2, CW])

        loaded, zeroed = sem("loaded3"), sem("zeroed3")
        step_done, std_done, spread_ready = sem("step_done"), sem("std_done"), sem("spread_ready")
        folded, k_done, cols_ready = sem("folded"), sem("k_done"), sem("cols_ready")
        h_loaded = [[sem(f"h_loaded{p}{i}") for i in range(PIECES)] for p in range(2)]
        sq_ready, sq_used = sem("sq_ready"), sem("sq_used")
        qs_ready, qt_done, qt_read = sem("qs_ready"), sem("qt_done"), sem("qt_read")
        var_ready, rstd_ready, shifted, exp_ready, w_ready = (sem(n) for n in ("var_ready", "rstd_ready", "shifted", "exp_ready", "w3_ready"))
        row_step = sem("row_step")
        wT_done, wT_ready, w_lo_ready = sem("wT_done"), sem("wT_ready"), sem("w_lo_ready")
        wb_done, pr_ready, pr_used = sem("wb_done"), sem("pr_ready"), sem("pr_used")
        o_ready, res_done, res_ready = sem("o_ready"), sem("res_done"), sem("res_ready")
        stored = [sem("stored0"), sem("stored1")]

        bank = lambda b, cols=CW, rows=P: psum[0:rows, b * BANK:b * BANK + cols]
        q_bank, qt_bank, wT_bank, o_bank, res_bank = bank(0), bank(1), bank(2, rows=TN), bank(5), bank(6, rows=T * D)
        wb_bank = lambda n: bank(3 + n % 2)
        k_bank = psum[:, 7 * BANK:8 * BANK]
        NBLK = TILES // CB
        sum_order = [j * QC + i for i in range(QC) for j in range(4) if j * QC + i < FC]
        half = FC // 2
        pool_order = [c for i in range(half + 1) for c in (i, half + 1 + i) if c < FC]
        AHEAD = 12
        block = ctx.enter_context(nc.Block())

        loads = [(ident[:], ins["ident"]), (fold[:], ins["fold"]), (quarter[:], ins["quarter"]),
                 (score_mask[:], ins["score_mask"]), (sum_mask[:], ins["sum_mask"]), (square_mask[:], ins["square_mask"]),
                 (pool_mask[:], ins["pool_mask"]), (spread_raw, ins["spread"]), (fold_out[:], ins["fold_out"]),
                 (par[:], ins["par"]), (aw[:], ins["aw"]), (ab[:], ins["attn_b"].partition_broadcast(P)),
                 (rowpar[:], ins["rowpar"]), (t_mask[:], ins["t_mask"])]

        @block.sync
        def _(sp):
            for dst, src in loads:
                sp.dma_start(dst, src).then_inc(loaded, 16)

            def load_h(i):
                p, width = i % 2, FC // PIECES
                for n in range(PIECES):
                    if i >= 2:
                        sp.wait_ge(pr_ready, FC * (i - 1))
                    cs = slice(n * width, (n + 1) * width)
                    for k in range(CB):
                        sp.dma_start(h[:, p, cs, k * P:(k + 1) * P], hF[i * CB + k, :, cs, :]).then_inc(h_loaded[p][n], 16)

            def store(sp, i):
                sp.wait_ge(res_ready, i + 1)
                sp.dma_start(out[:, i * CW:(i + 1) * CW], res[:, i % 2]).then_inc(stored[i % 2], 16)

            load_h(0)
            sp.wait_ge(spread_ready, 1)
            load_h(1)
            for i in range(2, NBLK):
                load_h(i)
                store(sp, i - 2)
            for i in (NBLK - 2, NBLK - 1):
                store(sp, i)
            for p in range(2):
                sp.wait_ge(stored[p], 16 * (NBLK // 2))

        @block.vector
        def _(dve):
            n = [0]

            def step(ins_):
                n[0] += 1
                ins_.then_inc(step_done, 1)
                dve.wait_ge(step_done, n[0])

            V = nc.vector
            by_node = lambda ap: ap.rearrange("p i c -> p c i")
            step(V.memset(ones[:], 1.0))
            step(V.memset(eps[:], EPS))
            step(V.memset(K[:], 0.0))
            step(V.memset(rowblk[:], 0.0))
            step(V.tensor_reduce(fsum[:, 0], by_node(means[:]), AX.X, ALU.add))
            assert n[0] == ST_MEAN
            dve.wait_ge(loaded, 16 * len(loads))
            step(V.tensor_tensor(LA[:], par[:, 2], aw[:].to_broadcast([P, FC]), ALU.mult))
            step(V.tensor_tensor(LBA[:], par[:, 3], aw[:].to_broadcast([P, FC]), ALU.mult))
            step(V.tensor_reduce(sums[:, 0:1], par[:, 1], AX.X, ALU.add))
            assert n[0] == ST_LA
            dve.wait_ge(folded, 1)
            step(V.tensor_scalar(mean_rep[:], k_bank[:, 0:TN], 1.0 / (4 * TILES), None, ALU.mult))
            step(V.tensor_tensor(mdev[:], means[:], mean_rep[:].unsqueeze(1).to_broadcast([P, TILES, TN]), ALU.subtract))
            step(V.tensor_tensor(mdev[:], mdev[:], mdev[:], ALU.mult))
            step(V.scalar_tensor_tensor(out=mdev[:], in0=mdev[:], scalar=32.0, in1=devs[:], op0=ALU.mult, op1=ALU.add))
            step(V.tensor_reduce(fsum[:, 1], by_node(mdev[:]), AX.X, ALU.add))
            assert n[0] == ST_VAR
            for q in range(FQ):
                rows = slice(D * q, D * q + D)
                step(V.tensor_copy(mu[rows, :], mean_rep[rows, q:TN:FQ]))
            dve.wait_ge(folded, 2)
            for q in range(FQ):
                rows = slice(D * q, D * q + D)
                step(V.tensor_copy(var[rows, :], k_bank[rows, TN + q:2 * TN:FQ]))
            assert n[0] == ST_VARF
            step(V.tensor_scalar(nmu[:], mu[:], -1.0, None, ALU.mult))
            dve.wait_ge(std_done, 1)
            step(V.reciprocal(inv[:], std[:]))
            step(V.tensor_tensor(A[:], par[:, 0], inv[:], ALU.mult))
            step(V.tensor_tensor(Amu[:], A[:], mu[:], ALU.mult))
            step(V.tensor_tensor(C[:], par[:, 1], Amu[:], ALU.subtract))
            step(V.tensor_reduce(sums[:, 1:2], C[:], AX.X, ALU.add))
            step(V.tensor_tensor(CLA[:], C[:], LA[:], ALU.mult))
            dve.wait_ge(k_done, 1)
            step(V.tensor_scalar(c0[:], k_bank[:, 3 * SW:3 * SW + 1], 1.0 / F, None, ALU.mult))
            step(V.tensor_scalar(Csq[:], C[:], c0[:], None, ALU.subtract))
            assert n[0] == ST_CSQ
            step(V.tensor_tensor(ALA[:], A[:], LA[:], ALU.mult))
            step(V.tensor_tensor(score_cols[:], score_mask[:], ALA[:].unsqueeze(2).to_broadcast([P, FC, D]), ALU.mult))
            step(V.tensor_tensor(sum_cols[:], sum_mask[:].unsqueeze(1).to_broadcast([P, FC, D]),
                                 A[:].unsqueeze(2).to_broadcast([P, FC, D]), ALU.mult))
            V.tensor_tensor(score_cols[:], score_cols[:], sum_cols[:], ALU.add).then_inc(cols_ready, 1)
            step(V.tensor_tensor(ALG[:], A[:], par[:, 2], ALU.mult))
            step(V.tensor_tensor(pool_cols[:, 0:FC], pool_mask[:, 0:FC], ALG[:].unsqueeze(2).to_broadcast([P, FC, D]), ALU.mult))
            step(V.tensor_tensor(pool_cols[:, FC], pool_mask[:, FC], ALG[:, half:half + 1].to_broadcast([P, D]), ALU.mult))
            step(V.tensor_tensor(rowpar[:, 0], rowpar[:, 0], rowpar[:, 1], ALU.mult))
            for t in range(T):
                step(V.tensor_tensor(rowblk[:, :, t], rowpar[:], t_mask[:, t:t + 1].unsqueeze(2).to_broadcast([TN, 3, D]), ALU.mult))
            dve.wait_ge(k_done, 2)
            step(V.tensor_copy(K[:, :, 0:TN], k_bank[:, 0:3 * SW].rearrange("p (k c) -> p k c", k=3)[:, :, 0:TN]))
            step(V.tensor_scalar(K[:, 1], K[:, 1], ab[:], None, ALU.add))
            V.tensor_copy(csum[:], k_bank[:, 3 * SW + 1:3 * SW + 2]).then_inc(cols_ready, 1)
            dve.wait_ge(cols_ready, 2)

            def per_row(ap, width=SW):
                return ap.unsqueeze(2).to_broadcast([P, CB, width])

            m = [0]

            def rstep(ins_):
                m[0] += 1
                ins_.then_inc(row_step, 1)
                dve.wait_ge(row_step, m[0])

            def softmax(i):
                dve.wait_ge(sq_used, FC * (i + 1))
                wait(dve, qt_done, i)
                V.tensor_copy(qs[:], q_bank).then_inc(qs_ready, 1)
                dve.wait_ge(qt_done, i + 1)
                rows = qt_bank.rearrange("p (s j r) -> p s j r", s=CB, j=4)
                s1, s2, nm, dm, dm2, v0, v1, std_, rs = (st[:, k] for k in range(9))
                rstep(V.tensor_reduce(s1, rows[:, :, :, QR], AX.X, ALU.add))
                rstep(V.tensor_reduce(s2, rows[:, :, :, QR + 1], AX.X, ALU.add))
                rstep(V.tensor_scalar(nm, s1, csum[:], -1.0 / F, ALU.add, ALU.mult))
                rstep(V.tensor_scalar(dm, nm, c0[:], None, ALU.add))
                rstep(V.tensor_tensor(dm2, dm, dm, ALU.mult))
                rstep(V.scalar_tensor_tensor(out=v0, in0=s2, scalar=1.0 / F, in1=dm2, op0=ALU.mult, op1=ALU.subtract))
                V.tensor_scalar(v1, v0, 0.0, None, ALU.max).then_inc(var_ready, 1)
                scores = lambda k: sc[:, k].rearrange("p s (j r) -> p s j r", j=4)
                V.tensor_tensor(scores(0), rows[:, :, :, 0:QR],
                                K[:, 2].rearrange("p (j r) -> p j r", j=4).unsqueeze(1).to_broadcast([P, CB, 4, QR]),
                                ALU.add).then_inc(qt_read, 1)
                rstep(V.tensor_tensor(sc[:, 1], K[:, 0:1].to_broadcast([P, CB, SW]), per_row(nm), ALU.mult))
                dve.wait_ge(qt_read, i + 1)
                rstep(V.tensor_tensor(sc[:, 0], sc[:, 0], sc[:, 1], ALU.add))
                dve.wait_ge(rstd_ready, i + 1)
                rstep(V.reciprocal(rs, std_))
                rstep(V.tensor_tensor(sc[:, 0], sc[:, 0], per_row(rs), ALU.mult))
                rstep(V.tensor_tensor(sc[:, 0], sc[:, 0], K[:, 1:2].to_broadcast([P, CB, SW]), ALU.add))
                nodes = lambda ap: ap.rearrange("p s (t n) -> p s t n", t=T)
                spread_t = lambda ap: ap.unsqueeze(3).to_broadcast([P, CB, T, N])
                live = nodes(sc[:, 0, :, 0:TN])
                rstep(V.tensor_reduce(mx[:, 0], live, AX.X, ALU.max))
                V.tensor_tensor(nodes(sc[:, 1, :, 0:TN]), live, spread_t(mx[:, 0]), ALU.subtract).then_inc(shifted, 1)
                dve.wait_ge(exp_ready, i + 1)
                ex = nodes(sc[:, 2, :, 0:TN])
                rstep(V.tensor_reduce(mx[:, 1], ex, AX.X, ALU.add))
                rstep(V.reciprocal(mx[:, 2], mx[:, 1]))
                rstep(V.tensor_tensor(nodes(w[:, 2]), ex, spread_t(mx[:, 2]), ALU.mult))
                rstep(V.tensor_tensor(w[:, 0], w[:, 2], per_row(rs, TN), ALU.mult))
                V.tensor_tensor(w[:, 1], w[:, 0], per_row(nm, TN), ALU.mult).then_inc(w_ready, 1)

            def pool(i):
                dve.wait_ge(wT_ready, 3 * i + 1)
                V.tensor_tensor(w_lo[:], wT[:, 0], w_hi[:].bitcast(fp32), ALU.subtract).then_inc(w_lo_ready, 1)
                for k, c in enumerate(pool_order):
                    g = i * FC + k
                    dve.wait_ge(wb_done, g + 1)
                    wait(dve, pr_used, g - 2)
                    V.scalar_tensor_tensor(out=pr[:, g % 3], in0=h[:, i % 2, c, :], scalar=nmu[:, c:c + 1], in1=wb_bank(g),
                                           op0=ALU.add, op1=ALU.mult).then_inc(pr_ready, 1)
                dve.wait_ge(pr_used, FC * (i + 1))
                V.tensor_copy(O_sb[:], o_bank).then_inc(o_ready, 1)

            def result(i):
                dve.wait_ge(res_done, i + 1)
                if i >= 2:
                    dve.wait_ge(stored[i % 2], 16 * (i // 2))
                V.tensor_copy(res[:, i % 2], res_bank).then_inc(res_ready, 1)

            for i in range(NBLK):
                softmax(i)
                if i:
                    result(i - 1)
                pool(i)
            result(NBLK - 1)

        @block.scalar
        def _(act):
            act.wait_ge(loaded, 16 * len(loads))
            nc.scalar.copy(spread[:].rearrange("p c f -> p (c f)"), spread_raw).then_inc(spread_ready, 1)
            act.wait_ge(step_done, ST_VARF)
            nc.scalar.activation(std[:], var[:], ACT.Sqrt, scale=1.0 / B, bias=eps[:]).then_inc(std_done, 1)
            act.wait_ge(step_done, ST_CSQ)

            def square(i, k):
                g, c = i * FC + k, sum_order[k]
                act.wait_ge(h_loaded[i % 2][c // (FC // PIECES)], 16 * CB * (i // 2 + 1))
                wait(act, sq_used, g - 3)
                nc.scalar.activation(sq[:, g % 4], h[:, i % 2, c, :], ACT.Square, bias=Csq[:, c:c + 1],
                                     scale=A[:, c:c + 1]).then_inc(sq_ready, 1)

            def copy_weights(i):
                for k in range(3):
                    act.wait_ge(wT_done, 3 * i + k + 1)
                    if k == 0:
                        wait(act, wb_done, FC * i)
                        wait(act, w_lo_ready, i)
                        wait(act, res_done, i)
                        nc.scalar.copy(w_hi[:], wT_bank)
                    nc.scalar.copy(wT[:, k], wT_bank).then_inc(wT_ready, 1)

            for k in range(FC):
                square(0, k)
            for i in range(NBLK):
                more = i + 1 < NBLK
                squares = list(range(FC)) if more else []
                for at, what in ((3, "std"), (9, "exp"), (AHEAD + 1, "weights")):
                    while squares and squares[0] < at:
                        square(i + 1, squares.pop(0))
                    if what == "std":
                        act.wait_ge(var_ready, i + 1)
                        nc.scalar.activation(st[:, 7], st[:, 6], ACT.Sqrt, bias=eps[:]).then_inc(rstd_ready, 1)
                    elif what == "exp":
                        act.wait_ge(shifted, i + 1)
                        nc.scalar.activation(sc[:, 2, :, 0:TN], sc[:, 1, :, 0:TN], ACT.Exp).then_inc(exp_ready, 1)
                    else:
                        copy_weights(i)
                while squares:
                    square(i + 1, squares.pop(0))

        @block.tensor
        def _(pe):
            MM = nc.tensor.matmul
            pe.wait_ge(loaded, 16 * len(loads))
            pe.wait_ge(step_done, ST_MEAN)
            MM(k_bank[:, 0:TN], fold[:], fsum[:, 0], start=True, stop=True).then_inc(folded, 1)
            pe.wait_ge(step_done, ST_VAR)
            MM(k_bank[:, TN:2 * TN], fold[:], fsum[:, 1], start=True, stop=True).then_inc(folded, 1)
            pe.wait_ge(step_done, ST_VARF)

            def k_row(k, src):
                for q in range(FQ):
                    MM(k_bank[:, k * SW + q:k * SW + q + FQ * (FC - 1) + 1:FQ], quarter[:, q], src[:], start=True, stop=True)

            k_row(0, LA)
            k_row(1, LBA)
            MM(k_bank[:, 3 * SW:3 * SW + 1], ones[:], sums[:, 0:1], start=True, stop=True).then_inc(k_done, 1)
            pe.wait_ge(step_done, ST_CSQ)
            k_row(2, CLA)
            MM(k_bank[:, 3 * SW + 1:3 * SW + 2], ones[:], sums[:, 1:2], start=True, stop=True).then_inc(k_done, 1)
            pe.wait_ge(cols_ready, 1)

            def sums_of(i, k):
                g, c = i * FC + k, sum_order[k]
                j = c // QC
                out_ = q_bank[D * j:D * j + D, :]
                if k == 0:
                    wait(pe, qs_ready, i)
                pe.wait_ge(h_loaded[i % 2][c // (FC // PIECES)], 16 * CB * (i // 2 + 1))
                MM(out_, score_cols[:, c], h[:, i % 2, c, :], start=c % QC == 0, stop=False)
                pe.wait_ge(sq_ready, g + 1)
                last = MM(out_, square_mask[:], sq[:, g % 4], start=False, stop=c % QC == QC - 1 or c == FC - 1)
                last.then_inc(sq_used, 1)

            def turn_sums(i):
                pe.wait_ge(qs_ready, i + 1)
                wait(pe, qt_read, i)
                for s in range(CB):
                    last = nc.tensor.transpose(qt_bank[:, s * P:(s + 1) * P], qs[:, s * P:(s + 1) * P], ident[:])
                last.then_inc(qt_done, 1)

            def turn_weights(i):
                pe.wait_ge(w_ready, i + 1)
                for k in range(3):
                    wait(pe, wT_ready, 3 * i + k)
                    for s in range(CB):
                        last = nc.tensor.transpose(wT_bank[:, s * P:(s + 1) * P], w[:, k, s], ident[:])
                    last.then_inc(wT_done, 1)

            def spread_weights(i, k):
                g, c = i * FC + k, pool_order[k]
                wait(pe, pr_ready, g - 1)
                MM(wb_bank(g), spread[:, c], w_lo[:], start=True, stop=False)
                MM(wb_bank(g), spread[:, c], w_hi[:], start=False, stop=True).then_inc(wb_done, 1)

            def pool_chunk(i, k):
                g, c = i * FC + k, pool_order[k]
                pe.wait_ge(pr_ready, g + 1)
                if k == 0:
                    wait(pe, o_ready, i)
                parts = [(0, c), (1, FC)] if c == half else [(int(c > half), c)]
                for t, col in parts:
                    j = 2 * t + c % 2
                    in_group = [x for x in pool_order if x % 2 == c % 2 and (x <= half if t == 0 else x >= half)]
                    last = MM(o_bank[D * j:D * j + D, :], pool_cols[:, col], pr[:, g % 3],
                              start=c == in_group[0], stop=c == in_group[-1])
                last.then_inc(pr_used, 1)

            def finish(i):
                last = None
                pe.wait_ge(o_ready, i + 1)
                pe.wait_ge(wT_ready, 3 * i + 3)
                wait(pe, res_ready, i)
                MM(res_bank, fold_out[:], O_sb[:], start=True, stop=False)
                for k in range(3):
                    last = MM(res_bank, rowblk[:, k].rearrange("p t d -> p (t d)"), wT[:, k], start=False, stop=k == 2)
                last.then_inc(res_done, 1)

            for k in range(FC):
                sums_of(0, k)
            turn_sums(0)
            for i in range(NBLK):
                left = list(range(FC)) if i + 1 < NBLK else []
                while left and left[0] < AHEAD:
                    sums_of(i + 1, left.pop(0))
                if i == 0:
                    pe.wait_ge(cols_ready, 2)
                turn_weights(i)
                pe.wait_ge(w_lo_ready, i + 1)
                for k in range(FC):
                    spread_weights(i, k)
                    if left and k % 2:
                        sums_of(i + 1, left.pop(0))
                    if k >= 2:
                        pool_chunk(i, k - 2)
                while left:
                    sums_of(i + 1, left.pop(0))
                pool_chunk(i, FC - 2)
                pool_chunk(i, FC - 1)
                if i + 1 < NBLK:
                    turn_sums(i + 1)
                finish(i)


ST_MEAN = 5
ST_LA = ST_MEAN + 3
ST_VAR = ST_LA + 5
ST_VARF = ST_VAR + 2 * FQ
ST_CSQ = ST_VARF + 9


def program(nc, ins, out):
    adjT = nc.dram_tensor("adjT", [TILES, N, TN, P], fp32, kind="Internal").ap()
    hF = nc.dram_tensor("hF", [TILES, P, FC, P], fp32, kind="Internal").ap()
    with nc.psum_tensor("psum", [P, 8 * BANK], fp32) as psum:
        stage1(nc, psum, ins["xT"], ins["W"], adjT, ins["ident"])
        with nc.sbuf_tensor("means", [P, TILES, TN], fp32) as means, nc.sbuf_tensor("devs", [P, TILES, TN], fp32) as devs:
            stage2(nc, psum, ins, adjT, hF, (means, devs))
            stage3(nc, psum, ins, hF, (means, devs), out)


def masks(np, dtype):
    q, d = np.divmod(np.arange(P), D)
    c, r, tn = np.arange(FC), np.arange(D), np.arange(TN)
    masker = (FQ * c[None, :] + q[:, None]) // N
    pool = (d[:, None, None] == r) & np.ones((P, FC + 1, 1), bool)
    mixed = FC // 2
    pool[:, mixed] &= (masker[:, mixed] == 0)[:, None]
    pool[:, FC] &= (masker[:, mixed] == 1)[:, None]
    found = {
        "score_mask": r == FQ * (c % QC)[None, :, None] + q[:, None, None],
        "sum_mask": (r == QR) & np.ones((P, 1), bool),
        "square_mask": (r == QR + 1) & np.ones((P, 1), bool),
        "pool_mask": pool,
        "quarter": (q[:, None, None] == np.arange(FQ)[:, None]) & np.ones((1, 1, P), bool),
        "spread": (tn[:, None, None] == FQ * c[:, None] + q).reshape(TN, FC * P),
        "fold_out": (q[:, None] // 2 == np.arange(T * D) // D) & (d[:, None] == np.arange(T * D) % D),
        "t_mask": tn[:, None] // N == np.arange(T),
    }
    return {name: a.astype(dtype) for name, a in found.items()}


def kernel(r_x, L0_rec_masker_param, L0_rec_masker_bias, L0_rec_weight, L0_rec_w_ih, L0_rec_w_hh, L0_rec_b_ih, L0_rec_b_hh,
           L0_rec_bn_gamma, L0_rec_bn_beta, L0_rec_ln_gamma, L0_rec_ln_beta, L0_rec_attn_w, L0_rec_attn_b):
    import numpy as np
    import concourse.bacc as bacc
    from concourse.bass_utils import run_bass_kernel_spmd

    x = np.asarray(r_x)
    to = lambda a: np.asarray(a)
    gates = np.stack([to(L0_rec_b_ih).reshape(3, D), to(L0_rec_b_hh).reshape(3, D)]).transpose(2, 0, 1)
    arrays = {
        "xT": np.concatenate([x.reshape(B, KX).T, np.ones((1, B), x.dtype)]),
        "W": np.concatenate([to(L0_rec_masker_param).transpose(1, 0, 2).reshape(KX, T * N * N),
                             to(L0_rec_masker_bias).reshape(1, T * N * N)]),
        "ident": np.eye(P, dtype=x.dtype),
        "fold": np.tile(np.eye(D, dtype=x.dtype), (4, 4)),
        "xm": x.transpose(1, 0, 2),
        "xg": x.reshape(TILES, 4, 32, N, D).transpose(0, 1, 4, 2, 3).reshape(TILES, P, 32, N),
        "wT4": np.tile(to(L0_rec_weight)[0].T, (1, 4)),
        "wihT": to(L0_rec_w_ih).T,
        "whhT4": np.tile(to(L0_rec_w_hh).T, (4, 1)),
        "biases": np.tile(gates, (4, 1, 1)),
        "par": np.stack([to(a).reshape(FC, FQ, D).transpose(1, 2, 0).reshape(P, FC)
                         for a in (L0_rec_bn_gamma, L0_rec_bn_beta, L0_rec_ln_gamma, L0_rec_ln_beta)], axis=1),
        "rowpar": np.stack([to(a).reshape(TN, D) for a in (L0_rec_bn_beta, L0_rec_ln_gamma, L0_rec_ln_beta)], axis=1),
        "aw": np.tile(to(L0_rec_attn_w).reshape(D, 1), (FQ, 1)),
        "attn_b": to(L0_rec_attn_b).reshape(1),
        **masks(np, x.dtype),
    }
    arrays = {name: np.ascontiguousarray(a) for name, a in arrays.items()}
    nc = bacc.Bacc("TRN2", target_bir_lowering=False, num_devices=1)
    ins = {name: nc.dram_tensor(name, a.shape, mybir.dt.from_np(a.dtype), kind="ExternalInput").ap() for name, a in arrays.items()}
    out = nc.dram_tensor("out", [T * D, B], fp32, kind="ExternalOutput").ap()
    program(nc, ins, out)
    result = run_bass_kernel_spmd(nc, [arrays], core_ids=[0])
    return np.ascontiguousarray(result.results[0]["out"].T)
```

```python
import concourse.bass as bass
from concourse import mybir
from contextlib import ExitStack

fp32 = mybir.dt.float32
fp32r = mybir.dt.float32r
ALU = mybir.AluOpType
ACT = mybir.ActivationFunctionType
AX = mybir.AxisListType

B, N, D, T = 2048, 50, 32, 2
TN = T * N
P = 128
TILES = B // P
KX = N * D
KF = KX // P
KR = KX - KF * P
assert 2 * KR == P
KC = KF + 1
BIAS_HI = KR + 32
KLAST = BIAS_HI + 1
GN = 10
GW = GN * N
GROUPS = T * N // GN
BLK = 8
BLOCKS = TILES // BLK
ITERS = BLOCKS * GROUPS
MPAD = 64
PAIRS = GN // 2
EPS_ROW = 1e-6
EPS = 1e-5
UNITS = [(u, min(u + 2, KC)) for u in range(0, KC, 2)]
NU = len(UNITS)
T_AT = 3

BANK = 512

QB = 4
ROUNDS = 32 // QB
RC = QB * TN
XPARTS = 4
XG = 32 // XPARTS
TPARTS = 4
TC = TN // TPARTS
LAST_V = 3 * TN // 5
R_G, Z_G, N_G = 0, 1, 2
FQ = P // D
FC = TN // FQ
F = TN * D
CB = 4
CW = CB * P
QC = (FC + 3) // 4
QR = FQ * QC


def wait(eng, sem, value):
    if not (isinstance(value, int) and value <= 0):
        eng.wait_ge(sem, value)


def stage1(nc, psum, xT, W, adjT, ident_d):
    with ExitStack() as ctx:
        sb = lambda name, shape, dt=fp32: ctx.enter_context(nc.sbuf_tensor(name, shape, dt))
        sem = lambda name: ctx.enter_context(nc.semaphore(name))
        x_hi = sb("x_hi", [P, KC, BLK * P], fp32r)
        x_lo = sb("x_lo", [P, KC, BLK * P], fp32r)
        x_raw = sb("x_raw", [P, KC + 1, P])
        w_hi = sb("w_hi", [P, KC, GW], fp32r)
        w_lo = sb("w_lo", [P, KC, GW], fp32r)
        w_raw = sb("w_raw", [P, KC + 1, GW])
        ident = sb("ident_sb", [P, P])
        u = sb("u", [P, 2, GN, N])
        an = sb("an", [P, 2, PAIRS, 2, MPAD])
        rows = sb("rows", [P, 3, GN])
        at = sb("at", [P, 2, PAIRS, P])

        x_loaded, ident_loaded = sem("x_loaded"), sem("ident_loaded")
        w_loaded = [sem(f"w_loaded{i}") for i in range(NU)]
        x_hi_ready, x_ready = sem("x_hi_ready"), sem("x_ready")
        w_hi_ready, w_ready, w_used = sem("w_hi_ready"), sem("w_ready"), sem("w_used")
        mm_done, u_ready, an_ready = sem("mm_done"), sem("u_ready"), sem("an_ready")
        tr_done, at_ready = sem("tr_done"), sem("at_ready")
        at_stored = [sem("at_stored0"), sem("at_stored1")]
        pad_zeroed, dve_step = sem("pad_zeroed"), sem("dve_step")

        def mm_out(c2):
            return psum[:, c2 * BANK:c2 * BANK + GW]

        def tr_out(c2):
            return psum[:, (2 + 2 * c2) * BANK:(2 + 2 * c2) * BANK + PAIRS * P]

        xT_main = xT[0:KC * P, :].rearrange("(k p) b -> p k b", p=P)
        W_main = W[0:KC * P, :].rearrange("(k p) n -> p k n", p=P)
        block = ctx.enter_context(nc.Block())

        @block.sync
        def _(sp):
            def load_x(bt):
                if bt >= 1:
                    sp.wait_ge(x_ready, bt)
                sp.dma_start(x_raw[:, 0:KC, :], xT_main[:, :, bt * P:(bt + 1) * P]).then_inc(x_loaded, 16)
                sp.dma_start(x_raw[0:KLAST, KC, :],
                             xT[KC * P:KC * P + KLAST, bt * P:(bt + 1) * P]).then_inc(x_loaded, 16)

            def load_w(i, group, after):
                k0, k1 = UNITS[i]
                if after is not None:
                    sp.wait_ge(w_ready, after)
                cols = bass.ds(group * GW, GW)
                sp.dma_start(w_raw[:, k0:k1, :], W_main[:, k0:k1, cols]).then_inc(w_loaded[i], 16)
                if i == NU - 1:
                    sp.dma_start(w_raw[0:KLAST, KC, :], W[KC * P:KC * P + KLAST, cols]).then_inc(w_loaded[i], 16)

            def store_tile(c, c2, tile, group):
                sp.wait_ge(at_ready, c + 1)
                for half in range(2):
                    sp.dma_start(adjT[tile, :, bass.ds(group * GN + half * PAIRS, PAIRS), :],
                                 at[MPAD * half:MPAD * half + N, c2, :, :]).then_inc(at_stored[c2], 16)

            load_x(0)
            for i in range(NU):
                load_w(i, 0, None)
                if i == 0:
                    sp.dma_start(ident[:, :], ident_d).then_inc(ident_loaded, 16)
            for blk in range(BLOCKS):
                for it, group in p1_iters(sp, blk):
                    for w in range(BLK):
                        if isinstance(it, int) and it == 0 and w + 1 < BLK:
                            load_x(w + 1)
                        if not (isinstance(it, int) and it == ITERS - 1):
                            nxt = 0 if isinstance(it, int) and it % GROUPS == GROUPS - 1 else group + 1
                            for i in range(NU):
                                if w == (min(i + 1, BLK - 2) if isinstance(it, int) and it == 0 else 1):
                                    load_w(i, nxt, it * NU + i + 1)
                        c = it * BLK + w
                        if w > 0:
                            store_tile(c - 1, (w - 1) % 2, blk * BLK + w - 1, group)
                        elif not (isinstance(it, int) and it == 0):
                            if isinstance(it, int) and it % GROUPS == 0:
                                store_tile(c - 1, 1, blk * BLK - 1, GROUPS - 1)
                            else:
                                store_tile(c - 1, 1, blk * BLK + BLK - 1, group - 1)
                        if isinstance(it, int) and it == GROUPS - 1 and blk + 1 < BLOCKS:
                            load_x(BLK + w)
            store_tile(ITERS * BLK - 1, 1, TILES - 1, GROUPS - 1)
            sp.wait_ge(at_stored[0], 32 * (ITERS * BLK // 2))
            sp.wait_ge(at_stored[1], 32 * (ITERS * BLK // 2))

        def split_x_hi(act, bt):
            act.wait_ge(x_loaded, 32 * (bt + 1))
            if bt >= BLK:
                act.wait_ge(mm_done, (GROUPS - 1) * BLK + bt - BLK + 1)
            cols = bass.ts(bt % BLK, P)
            nc.scalar.copy(x_hi[:, 0:KF, cols], x_raw[:, 0:KF, :])
            nc.scalar.copy(x_hi[0:KLAST, KF, cols], x_raw[0:KLAST, KC, :])
            nc.scalar.copy(x_lo[:, KF, cols], x_raw[:, KF, :]).then_inc(x_hi_ready, 1)

        def split_x_lo(dve, bt):
            dve.wait_ge(x_hi_ready, bt + 1)
            cols = bass.ts(bt % BLK, P)
            nc.vector.tensor_tensor(x_lo[:, 0:KF, cols], x_raw[:, 0:KF, :], x_hi[:, 0:KF, cols].bitcast(fp32), ALU.subtract)
            nc.vector.tensor_tensor(x_lo[KR:P, KF, cols], x_raw[KR:P, KF, :], x_lo[KR:P, KF, cols].bitcast(fp32),
                                    ALU.subtract).then_inc(x_ready, 1)

        def split_w_hi(act, i, it):
            act.wait_ge(w_loaded[i], (it + 1) * (32 if i == NU - 1 else 16))
            if not (isinstance(it, int) and it == 0):
                if i == NU - 1:
                    act.wait_ge(mm_done, it * BLK)
                else:
                    act.wait_ge(w_used, (it - 1) * (NU - 1) + i + 1)
            k0, k1 = UNITS[i]
            if i == NU - 1:
                nc.scalar.copy(w_lo[0:KLAST, KF, :], w_raw[0:KLAST, KC, :])
            nc.scalar.copy(w_hi[:, k0:k1, :], w_raw[:, k0:k1, :]).then_inc(w_hi_ready, 1)

        def split_w_lo(dve, i, it):
            dve.wait_ge(w_hi_ready, it * NU + i + 1)
            k0, k1 = UNITS[i]
            if i < NU - 1:
                nc.vector.tensor_tensor(w_lo[:, k0:k1, :], w_raw[:, k0:k1, :],
                                        w_hi[:, k0:k1, :].bitcast(fp32), ALU.subtract).then_inc(w_ready, 1)
            else:
                nc.vector.tensor_tensor(w_lo[0:BIAS_HI, KF, :], w_raw[0:BIAS_HI, KC, :],
                                        w_lo[0:BIAS_HI, KF, :].bitcast(fp32), ALU.subtract).then_inc(w_ready, 1)

        @block.scalar
        def _(act):
            def relu(c, c2, start=False):
                act.wait_ge(mm_done, c + 1)
                if not start:
                    act.wait_ge(an_ready, c - 1)
                nc.scalar.activation(u[:, c2].rearrange("p n m -> p (n m)"), mm_out(c2), ACT.Relu).then_inc(u_ready, 1)

            def evacuate(c, c2, start=False):
                act.wait_ge(tr_done, c + 1)
                if not start:
                    act.wait_ge(at_stored[c2], 16 * (c - c2))
                nc.scalar.copy(at[:, c2].rearrange("p q b -> p (q b)"), tr_out(c2)).then_inc(at_ready, 1)

            split_x_hi(act, 0)
            for i in range(NU):
                split_w_hi(act, i, 0)
            for blk in range(BLOCKS):
                for it, group in p1_iters(act, blk):
                    static = isinstance(it, int)
                    for w in range(BLK):
                        c = it * BLK + w
                        split = w == BLK - 1 and not (static and it == ITERS - 1)
                        if not (static and it == 0 and w == 0):
                            relu(c - 1, (w - 1) % 2, start=static and it == 0 and w <= 2)
                        if static and it == GROUPS and w == 0:
                            split_x_hi(act, 2 * BLK - 1)
                        if static and it == 0 and w + 1 < BLK:
                            split_x_hi(act, w + 1)
                        if split:
                            for i in range(0, T_AT + 1):
                                split_w_hi(act, i, it + 1)
                        if not (static and it == 0 and w == 0):
                            evacuate(c - 1, (w - 1) % 2, start=static and it == 0 and w <= 2)
                        if split:
                            for i in range(T_AT + 1, NU):
                                split_w_hi(act, i, it + 1)
                        if static and it == GROUPS - 1 and w >= 1:
                            split_x_hi(act, BLK + w - 1)
            c = ITERS * BLK - 1
            relu(c, 1)
            evacuate(c, 1)

        @block.vector
        def _(dve):
            nc.vector.memset(an[:].rearrange("p c q h m -> p (c q h m)"), 0.0).then_inc(pad_zeroed, 1)
            dve.wait_ge(pad_zeroed, 1)

            def normalise(c, c2, start=False):
                dve.wait_ge(u_ready, c + 1)
                nc.vector.tensor_reduce(rows[:, 0], u[:, c2], AX.X, ALU.add).then_inc(dve_step, 1)
                dve.wait_ge(dve_step, 3 * c + 1)
                nc.vector.tensor_scalar_add(rows[:, 1], rows[:, 0], EPS_ROW).then_inc(dve_step, 1)
                dve.wait_ge(dve_step, 3 * c + 2)
                nc.vector.reciprocal(rows[:, 2], rows[:, 1]).then_inc(dve_step, 1)
                dve.wait_ge(dve_step, 3 * c + 3)
                if not start:
                    dve.wait_ge(tr_done, c - 1)
                nc.vector.tensor_tensor(an[:, c2, :, :, 0:N].rearrange("p q h m -> p h q m"),
                                        u[:, c2].rearrange("p (h q) m -> p h q m", h=2),
                                        rows[:, 2].rearrange("p (h q) -> p h q", h=2).unsqueeze(3).to_broadcast([P, 2, PAIRS, N]),
                                        ALU.mult).then_inc(an_ready, 1)

            split_x_lo(dve, 0)
            for i in range(NU):
                split_w_lo(dve, i, 0)
            for blk in range(BLOCKS):
                for it, group in p1_iters(dve, blk):
                    static = isinstance(it, int)
                    for w in range(BLK):
                        c = it * BLK + w
                        if not (static and it == 0 and w == 0):
                            normalise(c - 1, (w - 1) % 2, start=static and it == 0 and w <= 2)
                        if static and it == GROUPS and w == 0:
                            split_x_lo(dve, 2 * BLK - 1)
                        if static and it == 0 and w + 1 < BLK:
                            split_x_lo(dve, w + 1)
                        if w == BLK - 1 and not (static and it == ITERS - 1):
                            for i in range(NU):
                                split_w_lo(dve, i, it + 1)
                        if static and it == GROUPS - 1 and w >= 1:
                            split_x_lo(dve, BLK + w - 1)
            normalise(ITERS * BLK - 1, 1)

        @block.tensor
        def _(pe):
            def transposes(c, c2, start=False):
                pe.wait_ge(an_ready, c + 1)
                if not start:
                    pe.wait_ge(at_ready, c - 1)
                for q in range(PAIRS):
                    last = nc.tensor.transpose(tr_out(c2)[:, q * P:(q + 1) * P],
                                               an[:, c2, q].rearrange("p h m -> p (h m)"), ident[:, :])
                last.then_inc(tr_done, 1)

            def window(it, w, blk, c, start=False, bank_free=False, none_before=False):
                pe.wait_ge(x_ready, blk * BLK + w + 1)
                if not bank_free:
                    pe.wait_ge(u_ready, c - 1)
                cols = bass.ts(w, P)
                for i, (k0, k1) in enumerate(UNITS):
                    if w == 0:
                        pe.wait_ge(w_ready, it * NU + i + 1)
                    for k in range(k0, k1):
                        if k < KF:
                            products = ((x_lo, w_hi, P), (x_hi, w_lo, P), (x_hi, w_hi, P))
                        else:
                            products = ((x_lo, w_hi, P), (x_hi, w_lo, KLAST))
                        for n, (a, b, r) in enumerate(products):
                            last = nc.tensor.matmul(mm_out(w % 2), a[0:r, k, cols], b[0:r, k, :],
                                                    start=k == 0 and n == 0, stop=k == KF and n == 1)
                    if i == NU - 1:
                        last.then_inc(mm_done, 1)
                    elif w == BLK - 1:
                        last.then_inc(w_used, 1)
                    if none_before and i == NU - 1:
                        pe.wait_ge(ident_loaded, 16)
                    if i == T_AT and not none_before:
                        transposes(c - 1, (w - 1) % 2, start=start)

            for blk in range(BLOCKS):
                for it, group in pe_iters(pe, blk):
                    static = isinstance(it, int)
                    for w in range(BLK):
                        c = it * BLK + w
                        window(it, w, blk, c, start=static and it == 0 and w <= 2,
                               bank_free=static and it == 0 and w < 2, none_before=static and it == 0 and w == 0)
            transposes(ITERS * BLK - 1, 1)


def p1_iters(eng, blk):
    base = blk * GROUPS
    yield base, 0
    with eng.Fori(1, GROUPS - 1) as g:
        yield base + g, g
    yield base + GROUPS - 1, GROUPS - 1


def pe_iters(eng, blk):
    base = blk * GROUPS
    if blk == 0:
        yield 0, 0
    with eng.Fori(1 if blk == 0 else 0, GROUPS) as g:
        yield base + g, g


def stage2(nc, psum, ins, adjT, hF, stats):
    with ExitStack() as ctx:
        sb = lambda name, shape, dt=fp32: ctx.enter_context(nc.sbuf_tensor(name, shape, dt))
        sem = lambda name: ctx.enter_context(nc.semaphore(name))
        adj = sb("adj_sb", [P, TN, P])
        xs = sb("xs_sb", [P, P, D])
        xg = sb("xg_sb", [P, 2, 32, N])
        xg_hi = sb("xg_hi", [P, 2, 32, N], fp32r)
        xg_lo = sb("xg_lo", [P, 2, 32, N], fp32r)
        hG = sb("hG", [P, 2, 32, TN])
        hT = sb("hT", [P, TN, D])
        hC = sb("hC", [P, FC, P])
        ident = sb("ident2_sb", [P, P])
        m_hi = sb("m_hi", [P, 2, RC], fp32r)
        m_lo = sb("m_lo", [P, 2, RC], fp32r)
        r_gate = sb("r_gate", [P, 2, RC])
        z_gate = sb("z_gate", [P, 2, RC])
        n_in = sb("n_in", [P, 2, RC])
        n_gate = sb("n_gate", [P, 2, RC])
        part = sb("part", [P, 8, TN])
        share = sb("share", [P, 1])
        wT4 = sb("wT4_sb", [D, P])
        wih = sb("wih_sb", [D, 3 * D])
        whh4 = sb("whh_sb", [P, 3 * D])
        biases = sb("biases_sb", [P, 2, 3])
        bias = sb("bias", [P, 3])
        wd = sb("wd", [P, 2, 3, P])
        wd_hi = sb("wd_hi", [P, 2, 3, P], fp32r)
        wd_lo = sb("wd_lo", [P, 2, 3, P], fp32r)
        means, devs = stats

        consts_loaded, ident_loaded = sem("consts_loaded"), sem("ident_loaded")
        g_product, zeroed, blocks_ready = sem("g_product"), sem("zeroed"), sem("blocks_ready")
        wd_hi_ready, wd_ready, bias_ready = sem("wd_hi_ready"), sem("wd_ready"), sem("bias_ready")
        adj_loaded = [sem("adj_loaded0"), sem("adj_loaded1")]
        xg_loaded = [sem("xg_loaded0"), sem("xg_loaded1")]
        xg_hi_ready, xg_ready = sem("xg_hi_ready"), sem("xg_ready")
        ax_done, m_hi_ready, m_ready = sem("ax_done"), sem("m_hi_ready"), sem("m_ready")
        gate_done = [sem(f"{g}_done") for g in ("r", "z", "n")]
        r_ready, z_ready, n_in_ready, n_ready = sem("r_ready"), sem("z_ready"), sem("n_in_ready"), sem("n_ready")
        d_step, h_ready = sem("d_step"), sem("h_ready")
        hT_ready = sem("hT_ready")
        turned, hC_ready, hC_stored = sem("turned"), sem("hC_ready"), sem("hC_stored")
        pool_step, share_ready, last_step = sem("pool_step"), sem("share_ready"), sem("last_step")
        hG_free = [sem("hG_free0"), sem("hG_free1")]

        S = 2 * ROUNDS
        ax_bank = lambda s: psum[:, (s % 2) * BANK:(s % 2) * BANK + RC]

        def gate_bank(gate, s):
            bank = {R_G: 2 + s % 2, N_G: 4 + s % 2, Z_G: 6}[gate]
            return psum[:, bank * BANK:bank * BANK + RC]

        turn_bank = psum[:, 7 * BANK:8 * BANK]
        batches = [(c, min(c + 4, FC)) for c in range(0, FC, 4)]
        assert len(batches) == ROUNDS - 1
        block = ctx.enter_context(nc.Block())

        @block.sync
        def _(sp):
            def load_adj(tile, r):
                sp.dma_start(adj[MPAD * r:MPAD * r + N, :, :], adjT[tile]).then_inc(adj_loaded[r], 16)
                sp.dma_start(xs[MPAD * r:MPAD * r + N, :, :],
                             ins["xm"][:, bass.ds(tile * P, P), :]).then_inc(adj_loaded[r], 16)

            def load_xg(tile, r):
                sp.dma_start(xg[:, r], ins["xg"][tile]).then_inc(xg_loaded[r], 16)

            def iteration(it, more):
                for r in range(2):
                    tile = it * 2 + r
                    if more:
                        sp.wait_ge(ax_done, (tile + 1) * ROUNDS)
                        load_adj(tile + 2, r)
                    if r or not (isinstance(it, int) and it == 0):
                        store(tile - 1)
                    sp.wait_ge(h_ready, (tile + 1) * ROUNDS)
                    if more:
                        load_xg(tile + 2, r)

            def store(tile):
                sp.wait_ge(hC_ready, (tile + 1) * len(batches))
                sp.dma_start(hF[tile], hC[:]).then_inc(hC_stored, 16)

            for dst, src in ((wT4, "wT4"), (wih, "wihT"), (whh4, "whhT4"), (biases, "biases")):
                sp.dma_start(dst[:], ins[src]).then_inc(consts_loaded, 16)
            load_xg(0, 0)
            load_adj(0, 0)
            sp.dma_start(ident[:], ins["ident"]).then_inc(ident_loaded, 16)
            load_xg(1, 1)
            load_adj(1, 1)
            iteration(0, True)
            with sp.Fori(1, TILES // 2 - 1) as it:
                iteration(it, True)
            iteration(TILES // 2 - 1, False)
            store(TILES - 1)
            sp.wait_ge(hC_stored, 16 * TILES)

        @block.scalar
        def _(act):
            act.wait_ge(blocks_ready, 1)
            nc.scalar.copy(wd_hi[:], wd[:]).then_inc(wd_hi_ready, 1)
            act.wait_ge(bias_ready, 1)

            def x_hi(it, r, k):
                if k == 0:
                    act.wait_ge(xg_loaded[r], (it + 1) * 16)
                    wait(act, gate_done[Z_G], it * S if r else it * S - ROUNDS)
                g = slice(k * XG, (k + 1) * XG)
                nc.scalar.copy(xg_hi[:, r, g], xg[:, r, g]).then_inc(xg_hi_ready, 1)

            def m_halves(it, s):
                act.wait_ge(ax_done, it * S + s + 1)
                nc.scalar.copy(m_hi[:, s % 2], ax_bank(s)).then_inc(m_hi_ready, 1)

            def evacuate(tile, n):
                act.wait_ge(turned, tile * len(batches) + n + 1)
                if n == 0:
                    wait(act, hC_stored, 16 * tile)
                c0, c1 = batches[n]
                nc.scalar.copy(hC[:, c0:c1, :].rearrange("p c b -> p (c b)"),
                               turn_bank[:, 0:(c1 - c0) * P]).then_inc(hC_ready, 1)

            def turn(it, more):
                for s in range(S):
                    r, q = divmod(s, ROUNDS)
                    if q and (r or not (isinstance(it, int) and it == 0)):
                        evacuate(it * 2 + r - 1, q - 1)
                    if s + 1 < S or more:
                        wait(act, gate_done[Z_G], it * S + s)
                        m_halves(it + (s + 1) // S, (s + 1) % S)
                    k = s % ROUNDS - (ROUNDS - 1 - XPARTS)
                    if 0 <= k < XPARTS and (s < ROUNDS or more):
                        x_hi(it + s // ROUNDS, 1 - s // ROUNDS, k)
                    act.wait_ge(gate_done[R_G], it * S + s + 1)
                    wait(act, h_ready, it * S + s - 1)
                    nc.scalar.activation(r_gate[:, s % 2], gate_bank(R_G, s), ACT.Sigmoid,
                                         bias=bias[:, R_G:R_G + 1]).then_inc(r_ready, 1)
                    act.wait_ge(gate_done[Z_G], it * S + s + 1)
                    nc.scalar.activation(z_gate[:, s % 2], gate_bank(Z_G, s), ACT.Sigmoid,
                                         bias=bias[:, Z_G:Z_G + 1]).then_inc(z_ready, 1)
                    act.wait_ge(n_in_ready, it * S + s + 1)
                    nc.scalar.activation(n_gate[:, s % 2], n_in[:, s % 2], ACT.Tanh).then_inc(n_ready, 1)

            for k in range(XPARTS):
                x_hi(0, 0, k)
            m_halves(0, 0)
            turn(0, True)
            with act.Fori(1, TILES // 2 - 1) as it:
                turn(it, True)
            turn(TILES // 2 - 1, False)
            for n in range(len(batches)):
                evacuate(TILES - 1, n)

        @block.vector
        def _(dve):
            nc.vector.memset(wd[:], 0.0).then_inc(zeroed, 1)
            dve.wait_ge(zeroed, 1)
            dve.wait_ge(consts_loaded, 64)
            dve.wait_ge(g_product, 1)
            for j in range(4):
                q = slice(D * j, D * j + D)
                nc.vector.tensor_copy(wd[q, 0, :, q], psum[q, 0:3 * D].rearrange("p (g e) -> p g e", g=3))
                last = nc.vector.tensor_copy(wd[q, 1, :, q], whh4[q, :].rearrange("p (g e) -> p g e", g=3))
            last.then_inc(blocks_ready, 1)
            nc.vector.tensor_tensor(bias[:], biases[:, 0], biases[:, 1], ALU.add).then_inc(bias_ready, 1)
            dve.wait_ge(wd_hi_ready, 1)
            nc.vector.tensor_tensor(wd_lo[:], wd[:], wd_hi[:].bitcast(fp32), ALU.subtract).then_inc(wd_ready, 1)
            dve.wait_ge(bias_ready, 1)

            def x_lo(it, r, k):
                dve.wait_ge(xg_hi_ready, (it * 2 + r) * XPARTS + k + 1)
                g = slice(k * XG, (k + 1) * XG)
                nc.vector.tensor_tensor(xg_lo[:, r, g], xg[:, r, g], xg_hi[:, r, g].bitcast(fp32),
                                        ALU.subtract).then_inc(xg_ready, 1)

            def m_halves(it, s):
                dve.wait_ge(m_hi_ready, it * S + s + 1)
                nc.vector.tensor_tensor(m_lo[:, s % 2], ax_bank(s), m_hi[:, s % 2].bitcast(fp32),
                                        ALU.subtract).then_inc(m_ready, 1)

            def nodes(ap):
                return ap.rearrange("p (g t n) -> p g t n", g=QB, t=T)

            def update(it, s):
                dve.wait_ge(gate_done[N_G], it * S + s + 1)
                dve.wait_ge(r_ready, it * S + s + 1)
                nc.vector.scalar_tensor_tensor(out=n_in[:, s % 2], in0=gate_bank(N_G, s), scalar=bias[:, N_G:N_G + 1],
                                               in1=r_gate[:, s % 2], op0=ALU.add, op1=ALU.mult).then_inc(n_in_ready, 1)

            def finish(it, s):
                r, q = divmod(s, ROUNDS)
                base = (it * S + s) * 2
                dve.wait_ge(n_ready, it * S + s + 1)
                diff = n_in[:, s % 2]
                x_b = xg[:, r, q * QB:(q + 1) * QB, :].unsqueeze(2).to_broadcast([P, QB, T, N])
                nc.vector.tensor_tensor(nodes(diff), x_b, nodes(n_gate[:, s % 2]), ALU.subtract).then_inc(d_step, 1)
                dve.wait_ge(d_step, base + 1)
                dve.wait_ge(z_ready, it * S + s + 1)
                nc.vector.tensor_tensor(diff, diff, z_gate[:, s % 2], ALU.mult).then_inc(d_step, 1)
                dve.wait_ge(d_step, base + 2)
                nc.vector.tensor_tensor(hG[:, r, q * QB:(q + 1) * QB, :].rearrange("p g c -> p (g c)"), diff,
                                        n_gate[:, s % 2], ALU.add).then_inc(h_ready, 1)

            def turn_rows(it, r, k):
                tile = it * 2 + r
                if k == 0:
                    dve.wait_ge(h_ready, (tile + 1) * ROUNDS)
                    wait(dve, turned, tile * len(batches))
                c = slice(k * TC, (k + 1) * TC)
                nc.vector.transpose(hT[:, c], hG[:, r, :, c].rearrange("p g c -> p c g")).then_inc(hT_ready, 1)

            def turn(it, more):
                for s in range(S):
                    if s + 1 < S or more:
                        m_halves(it + (s + 1) // S, (s + 1) % S)
                    k = s % ROUNDS - (ROUNDS - 1 - XPARTS)
                    if 0 <= k < XPARTS and (s < ROUNDS or more):
                        x_lo(it + s // ROUNDS, 1 - s // ROUNDS, k)
                    update(it, s)
                    if s % ROUNDS == 0:
                        wait(dve, hG_free[s // ROUNDS], it)
                    finish(it, s)
                    r, q = divmod(s, ROUNDS)
                    if q == ROUNDS - 1:
                        turn_rows(it, r, 0)
                    elif q < TPARTS - 1 and r:
                        turn_rows(it, 0, q + 1)
                    elif q < TPARTS - 1 and not (isinstance(it, int) and it == 0):
                        turn_rows(it - 1, 1, q + 1)

            for k in range(XPARTS):
                x_lo(0, 0, k)
            m_halves(0, 0)
            turn(0, True)
            with dve.Fori(1, TILES // 2 - 1) as it:
                turn(it, True)
            turn(TILES // 2 - 1, False)
            for k in range(1, TPARTS):
                turn_rows(TILES // 2 - 1, 1, k)
            h, mean, dev = hG[:, 1, :, 0:LAST_V], means[:, TILES - 1:, 0:LAST_V], devs[:, TILES - 1, 0:LAST_V]
            by_node = h.rearrange("p g c -> p c g")
            nc.vector.tensor_reduce(means[:, TILES - 1, 0:LAST_V], by_node, AX.X, ALU.add).then_inc(last_step, 1)
            dve.wait_ge(last_step, 1)
            nc.vector.tensor_scalar(mean, mean, 1.0 / 32, None, ALU.mult).then_inc(last_step, 1)
            dve.wait_ge(last_step, 2)
            dve.wait_ge(hT_ready, TILES * TPARTS)
            nc.vector.tensor_tensor(h, h, mean.to_broadcast([P, 32, LAST_V]), ALU.subtract).then_inc(last_step, 1)
            dve.wait_ge(last_step, 3)
            nc.vector.tensor_tensor(h, h, h, ALU.mult).then_inc(last_step, 1)
            dve.wait_ge(last_step, 4)
            nc.vector.tensor_reduce(dev, by_node, AX.X, ALU.add)

        @block.gpsimd
        def _(pool):
            TT = nc.gpsimd.tensor_tensor
            nc.gpsimd.memset(share[:], 1.0 / 32).then_inc(share_ready, 1)
            pool.wait_ge(share_ready, 1)

            def statistics(it, r, first=0):
                tile = it * 2 + r
                step = [tile * 14]

                def chain(ins_):
                    step[0] = step[0] + 1
                    ins_.then_inc(pool_step, 1)
                    pool.wait_ge(pool_step, step[0])

                h, p = hG[:, r, :, first:], part[:, :, first:]
                mean = p[:, 1:2]
                pool.wait_ge(h_ready, (tile + 1) * ROUNDS)
                chain(TT(p, h[:, 0:8], h[:, 8:16], ALU.add))
                chain(TT(p, p, h[:, 16:24], ALU.add))
                chain(TT(p, p, h[:, 24:32], ALU.add))
                for g in (4, 2, 1):
                    chain(TT(p[:, 0:g], p[:, 0:g], p[:, g:2 * g], ALU.add))
                for to in (mean, means[:, bass.ds(tile, 1), first:]):
                    chain(TT(to, p[:, 0:1], share[:].unsqueeze(1).to_broadcast([P, 1, TN - first]), ALU.mult))
                pool.wait_ge(hT_ready, (tile + 1) * TPARTS)
                chain(TT(h, h, mean.to_broadcast([P, 32, TN - first]), ALU.subtract))
                chain(TT(h, h, h, ALU.mult))
                for g in (16, 8, 4, 2):
                    chain(TT(h[:, 0:g], h[:, 0:g], h[:, g:2 * g], ALU.add))
                TT(devs[:, bass.ds(tile, 1), first:], h[:, 0:1], h[:, 1:2], ALU.add).then_inc(hG_free[r], 1)
                pool.wait_ge(hG_free[r], it + 1)

            with pool.Fori(0, TILES // 2 - 1) as it:
                statistics(it, 0)
                statistics(it, 1)
            statistics(TILES // 2 - 1, 0)
            statistics(TILES // 2 - 1, 1, LAST_V)

        @block.tensor
        def _(pe):
            pe.wait_ge(consts_loaded, 64)
            nc.tensor.matmul(psum[:, 0:3 * D], wT4[:], wih[:], start=True, stop=True).then_inc(g_product, 1)
            pe.wait_ge(wd_ready, 1)

            def aggregate(s):
                r, q = divmod(s, ROUNDS)
                rows = slice(MPAD * r, MPAD * r + N)
                for gi in range(QB):
                    for j in range(4):
                        b = 32 * j + q * QB + gi
                        last = nc.tensor.matmul(ax_bank(s)[D * j:D * j + D, gi * TN:(gi + 1) * TN],
                                                xs[rows, b, :], adj[rows, :, b], start=True, stop=True)
                last.then_inc(ax_done, 1)

            def gates(it, s, more):
                r, q = divmod(s, ROUNDS)
                if q == 0:
                    pe.wait_ge(xg_ready, (it * 2 + r + 1) * XPARTS)
                if s == ROUNDS - 2:
                    pe.wait_ge(adj_loaded[1], (it + 1) * 32)
                if s == S - 2 and more:
                    pe.wait_ge(adj_loaded[0], (it + 2) * 32)
                pe.wait_ge(m_ready, it * S + s + 1)
                xb = [t[:, r, q * QB:(q + 1) * QB, :].unsqueeze(2).to_broadcast([P, QB, T, N]) for t in (xg_hi, xg_lo)]
                for gate in (R_G, N_G, Z_G):
                    if gate == Z_G:
                        if q and (r or not (isinstance(it, int) and it == 0)):
                            turn_chunks(it * 2 + r - 1, q - 1)
                        wait(pe, z_ready, it * S + s)
                    else:
                        wait(pe, n_in_ready if gate == N_G else r_ready, it * S + s - 1)
                    terms = []
                    for part, (hi, lo) in enumerate(((m_hi[:, s % 2], m_lo[:, s % 2]), xb)):
                        terms += [(wd_lo[:, part, gate], hi), (wd_hi[:, part, gate], lo), (wd_hi[:, part, gate], hi)]
                    for i, (w, m) in enumerate(terms):
                        last = nc.tensor.matmul(gate_bank(gate, s), w, m, start=i == 0, stop=i == len(terms) - 1)
                    last.then_inc(gate_done[gate], 1)

            def turn_chunks(tile, n):
                c0, c1 = batches[n]
                pe.wait_ge(hT_ready, tile * TPARTS + (c1 * FQ + TC - 1) // TC)
                wait(pe, hC_ready, tile * len(batches) + n)
                features = hT[:].rearrange("p c d -> p (c d)")
                for c in range(c0, c1):
                    last = nc.tensor.transpose(turn_bank[:, (c - c0) * P:(c - c0 + 1) * P],
                                               features[:, c * P:(c + 1) * P], ident[:])
                last.then_inc(turned, 1)

            def turn(it, more):
                for s in range(S):
                    if s + 1 < S or more:
                        aggregate((s + 1) % S)
                    gates(it, s, more)

            pe.wait_ge(adj_loaded[0], 32)
            aggregate(0)
            pe.wait_ge(ident_loaded, 16)
            turn(0, True)
            with pe.Fori(1, TILES // 2 - 1) as it:
                turn(it, True)
            turn(TILES // 2 - 1, False)
            for n in range(len(batches)):
                turn_chunks(TILES - 1, n)


def stage3(nc, psum, ins, hF, stats, out):
    with ExitStack() as ctx:
        sb = lambda name, shape, dt=fp32: ctx.enter_context(nc.sbuf_tensor(name, shape, dt))
        sem = lambda name: ctx.enter_context(nc.semaphore(name))
        means, devs = stats
        SW = 4 * QR
        ident = sb("ident3_sb", [P, P])
        fold = sb("fold_sb", [P, P])
        quarter = sb("quarter_sb", [P, FQ, P])
        ones = sb("ones_sb", [P, P])
        score_mask = sb("score_mask_sb", [P, FC, D])
        square_mask = sb("square_mask_sb", [P, D])
        pool_mask = sb("pool_mask_sb", [P, FC + 1, D])
        spread = sb("spread_sb", [TN, FC, P], fp32r)
        fold_out = sb("fold_out_sb", [P, T * D])
        par = sb("par_sb", [P, 4, FC])
        aw = sb("awF_sb", [P, 1])
        ab = sb("abF_sb", [P, 1])
        rowpar = sb("rowpar_sb", [TN, 3, D])
        t_mask = sb("t_mask_sb", [TN, T])
        rowblk = sb("rowblk", [TN, 3, T, D])
        eps = sb("eps3", [P, 1])
        fsum = sb("fsum", [P, 2, TN])
        mean_rep = sb("mean_rep", [P, TN])
        mdev = sb("mdev", [P, TILES, TN])
        mu, var, std, inv = (sb(n, [P, FC]) for n in ("mu_sb", "var_sb", "bnstd_sb", "inv_sb"))
        nmu, A, Amu, C, Csq = (sb(n, [P, FC]) for n in ("nmu_sb", "A_sb", "Amu_sb", "C_sb", "Csq_sb"))
        LA, ALA, CLA, LBA, ALG = (sb(n, [P, FC]) for n in ("LA_sb", "ALA_sb", "CLA_sb", "LBA_sb", "ALG_sb"))
        sums = sb("sums_sb", [P, 2])
        c0 = sb("c0_sb", [P, 1])
        csum = sb("csum_sb", [P, 1])
        score_cols = sb("score_cols", [P, FC, D])
        pool_cols = sb("pool_cols", [P, FC + 1, D])
        K = sb("K_sb", [P, 3, SW])
        h = sb("h3", [P, 2, FC, CW])
        spread_raw = h[0:TN, 1].rearrange("p c b -> p (c b)")[:, 0:FC * P]
        sq = sb("sq3", [P, 4, CW])
        pr = sb("pr3", [P, 3, CW])
        qs = sb("qs", [P, CW])
        st = sb("row_stats", [P, 9, CB])
        sc = sb("sc3", [P, 3, CB, SW])
        mx = sb("mx3", [P, 3, CB, T])
        w = sb("w3", [P, 3, CB, TN])
        wT = sb("wT3", [TN, 3, CW])
        w_hi = sb("w_hi3", [TN, CW], fp32r)
        w_lo = sb("w_lo3", [TN, CW], fp32r)
        O_sb = sb("O_sb", [P, CW])
        res = sb("res3", [T * D, 2, CW])

        loaded, fold_loaded = sem("loaded3"), sem("fold_loaded")
        step_done, std_done, spread_ready = sem("step_done"), sem("std_done"), sem("spread_ready")
        folded, k_done, cols_ready = sem("folded"), sem("k_done"), sem("cols_ready")
        h_loaded = [[sem(f"h_loaded{p}{i}") for i in range(QC)] for p in range(2)]
        sq_ready, sq_used = sem("sq_ready"), sem("sq_used")
        qs_ready, qt_done, qt_read = sem("qs_ready"), sem("qt_done"), sem("qt_read")
        var_ready, rstd_ready, shifted, exp_ready, w_ready = (sem(n) for n in ("var_ready", "rstd_ready", "shifted", "exp_ready", "w3_ready"))
        row_step = sem("row_step")
        wT_done, wT_ready, w_lo_ready = sem("wT_done"), sem("wT_ready"), sem("w_lo_ready")
        wb_done, pr_ready, pr_used = sem("wb_done"), sem("pr_ready"), sem("pr_used")
        o_ready, res_done, res_ready = sem("o_ready"), sem("res_done"), sem("res_ready")
        stored = [sem("stored0"), sem("stored1")]

        bank = lambda b, cols=CW, rows=P: psum[0:rows, b * BANK:b * BANK + cols]
        q_bank, qt_bank, o_bank, res_bank = bank(0), bank(1), bank(5), bank(6, rows=T * D)
        wT_bank = lambda n: bank((2, 7)[n % 2], rows=TN)
        wb_bank = lambda n: bank(3 + n % 2)
        k_bank = psum[:, 7 * BANK:8 * BANK]
        NBLK = TILES // CB
        order = [j * QC + i for i in range(QC) for j in range(4) if j * QC + i < FC]
        half = FC // 2
        ahead = lambda i: (18 if i == 0 else 4) if i + 1 < NBLK else 0
        POOL_FIRST = 11
        block = ctx.enter_context(nc.Block())

        loads = [(ident[:], ins["ident"]), (quarter[:], ins["quarter"]),
                 (score_mask[:], ins["score_mask"]), (square_mask[:], ins["square_mask"]),
                 (pool_mask[:], ins["pool_mask"]), (spread_raw, ins["spread"]), (fold_out[:], ins["fold_out"]),
                 (par[:], ins["par"]), (aw[:], ins["aw"]), (ab[:], ins["attn_b"].partition_broadcast(P)),
                 (rowpar[:], ins["rowpar"]), (t_mask[:], ins["t_mask"])]

        @block.sync
        def _(sp):
            sp.dma_start(fold[:], ins["fold"]).then_inc(fold_loaded, 16)
            for dst, src in loads:
                sp.dma_start(dst, src).then_inc(loaded, 16)

            def load_h(i):
                p = i % 2
                for n in range(QC):
                    cs = slice(n, FC, QC)
                    if i >= 2:
                        sp.wait_ge(pr_ready, FC * (i - 2) + 1 + max(order.index(c) for c in range(n, FC, QC)))
                    for k in range(CB):
                        sp.dma_start(h[:, p, cs, k * P:(k + 1) * P], hF[i * CB + k, :, cs, :]).then_inc(h_loaded[p][n], 16)

            def store(sp, i):
                sp.wait_ge(res_ready, i + 1)
                sp.dma_start(out[:, i * CW:(i + 1) * CW], res[:, i % 2]).then_inc(stored[i % 2], 16)

            load_h(0)
            sp.wait_ge(spread_ready, 1)
            load_h(1)
            for i in range(2, NBLK):
                load_h(i)
                store(sp, i - 2)
            for i in (NBLK - 2, NBLK - 1):
                store(sp, i)
            for p in range(2):
                sp.wait_ge(stored[p], 16 * (NBLK // 2))

        @block.vector
        def _(dve):
            n = [0]

            def step(ins_):
                n[0] += 1
                ins_.then_inc(step_done, 1)
                dve.wait_ge(step_done, n[0])

            V = nc.vector
            by_node = lambda ap: ap.rearrange("p i c -> p c i")
            step(V.memset(ones[:], 1.0))
            step(V.memset(eps[:], EPS))
            step(V.memset(K[:], 0.0))
            step(V.memset(rowblk[:], 0.0))
            step(V.tensor_reduce(fsum[:, 0], by_node(means[:]), AX.X, ALU.add))
            assert n[0] == ST_MEAN
            dve.wait_ge(folded, 1)
            step(V.tensor_scalar(mean_rep[:], k_bank[:, 0:TN], 1.0 / (4 * TILES), None, ALU.mult))
            step(V.tensor_tensor(mdev[:], means[:], mean_rep[:].unsqueeze(1).to_broadcast([P, TILES, TN]), ALU.subtract))
            step(V.tensor_tensor(mdev[:], mdev[:], mdev[:], ALU.mult))
            step(V.scalar_tensor_tensor(out=mdev[:], in0=mdev[:], scalar=32.0, in1=devs[:], op0=ALU.mult, op1=ALU.add))
            step(V.tensor_reduce(fsum[:, 1], by_node(mdev[:]), AX.X, ALU.add))
            assert n[0] == ST_VAR
            dve.wait_ge(loaded, 16 * len(loads))
            step(V.tensor_tensor(LA[:], par[:, 2], aw[:].to_broadcast([P, FC]), ALU.mult))
            step(V.tensor_tensor(LBA[:], par[:, 3], aw[:].to_broadcast([P, FC]), ALU.mult))
            step(V.tensor_reduce(sums[:, 0:1], par[:, 1], AX.X, ALU.add))
            assert n[0] == ST_LA
            for q in range(FQ):
                rows = slice(D * q, D * q + D)
                step(V.tensor_copy(mu[rows, :], mean_rep[rows, q:TN:FQ]))
            dve.wait_ge(folded, 2)
            for q in range(FQ):
                rows = slice(D * q, D * q + D)
                step(V.tensor_copy(var[rows, :], k_bank[rows, TN + q:2 * TN:FQ]))
            assert n[0] == ST_VARF
            step(V.tensor_scalar(nmu[:], mu[:], -1.0, None, ALU.mult))
            dve.wait_ge(std_done, 1)
            step(V.reciprocal(inv[:], std[:]))
            step(V.tensor_tensor(A[:], par[:, 0], inv[:], ALU.mult))
            step(V.tensor_tensor(Amu[:], A[:], mu[:], ALU.mult))
            step(V.tensor_tensor(C[:], par[:, 1], Amu[:], ALU.subtract))
            step(V.tensor_reduce(sums[:, 1:2], C[:], AX.X, ALU.add))
            step(V.tensor_tensor(CLA[:], C[:], LA[:], ALU.mult))
            dve.wait_ge(k_done, 1)
            step(V.tensor_scalar(c0[:], k_bank[:, 3 * SW:3 * SW + 1], 1.0 / F, None, ALU.mult))
            step(V.tensor_scalar(Csq[:], C[:], c0[:], None, ALU.subtract))
            assert n[0] == ST_CSQ
            step(V.tensor_tensor(ALA[:], A[:], LA[:], ALU.mult))
            step(V.tensor_tensor(score_cols[:], score_mask[:], ALA[:].unsqueeze(2).to_broadcast([P, FC, D]), ALU.mult))
            V.tensor_copy(score_cols[:, :, QR:QR + 1], A[:].unsqueeze(2)).then_inc(cols_ready, 1)
            step(V.tensor_tensor(ALG[:], A[:], par[:, 2], ALU.mult))
            step(V.tensor_tensor(pool_cols[:, 0:FC], pool_mask[:, 0:FC], ALG[:].unsqueeze(2).to_broadcast([P, FC, D]), ALU.mult))
            step(V.tensor_tensor(pool_cols[:, FC], pool_mask[:, FC], ALG[:, half:half + 1].to_broadcast([P, D]), ALU.mult))
            step(V.tensor_tensor(rowpar[:, 0], rowpar[:, 0], rowpar[:, 1], ALU.mult))
            for t in range(T):
                step(V.tensor_tensor(rowblk[:, :, t], rowpar[:], t_mask[:, t:t + 1].unsqueeze(2).to_broadcast([TN, 3, D]), ALU.mult))
            dve.wait_ge(k_done, 2)
            step(V.tensor_copy(K[:, :, 0:TN], k_bank[:, 0:3 * SW].rearrange("p (k c) -> p k c", k=3)[:, :, 0:TN]))
            step(V.tensor_scalar(K[:, 1], K[:, 1], ab[:], None, ALU.add))
            V.tensor_copy(csum[:], k_bank[:, 3 * SW + 1:3 * SW + 2]).then_inc(cols_ready, 1)
            dve.wait_ge(cols_ready, 2)

            def per_row(ap, width=SW):
                return ap.unsqueeze(2).to_broadcast([P, CB, width])

            m = [0]

            def rstep(ins_):
                m[0] += 1
                ins_.then_inc(row_step, 1)

            def last_step():
                dve.wait_ge(row_step, m[0])

            def softmax(i):
                dve.wait_ge(sq_used, FC * (i + 1))
                wait(dve, qt_done, i)
                V.tensor_copy(qs[:], q_bank).then_inc(qs_ready, 1)
                yield
                dve.wait_ge(qt_done, i + 1)
                rows = qt_bank.rearrange("p (s j r) -> p s j r", s=CB, j=4)
                s1, s2, nm, dm, dm2, v0, v1, std_, rs = (st[:, k] for k in range(9))
                rstep(V.tensor_reduce(s1, rows[:, :, :, QR], AX.X, ALU.add))
                yield
                last_step()
                rstep(V.tensor_reduce(s2, rows[:, :, :, QR + 1], AX.X, ALU.add))
                yield
                last_step()
                rstep(V.tensor_scalar(nm, s1, csum[:], -1.0 / F, ALU.add, ALU.mult))
                yield
                last_step()
                rstep(V.tensor_scalar(dm, nm, c0[:], None, ALU.add))
                yield
                last_step()
                rstep(V.tensor_tensor(dm2, dm, dm, ALU.mult))
                yield
                last_step()
                rstep(V.scalar_tensor_tensor(out=v0, in0=s2, scalar=1.0 / F, in1=dm2, op0=ALU.mult, op1=ALU.subtract))
                yield
                last_step()
                V.tensor_scalar(v1, v0, 0.0, None, ALU.max).then_inc(var_ready, 1)
                yield
                scores = lambda k: sc[:, k].rearrange("p s (j r) -> p s j r", j=4)
                V.tensor_tensor(scores(0), rows[:, :, :, 0:QR],
                                K[:, 2].rearrange("p (j r) -> p j r", j=4).unsqueeze(1).to_broadcast([P, CB, 4, QR]),
                                ALU.add).then_inc(qt_read, 1)
                yield
                rstep(V.tensor_tensor(sc[:, 1], K[:, 0:1].to_broadcast([P, CB, SW]), per_row(nm), ALU.mult))
                yield
                last_step()
                dve.wait_ge(qt_read, i + 1)
                rstep(V.tensor_tensor(sc[:, 0], sc[:, 0], sc[:, 1], ALU.add))
                yield
                last_step()
                dve.wait_ge(rstd_ready, i + 1)
                rstep(V.reciprocal(rs, std_))
                yield
                last_step()
                rstep(V.tensor_tensor(sc[:, 0], sc[:, 0], per_row(rs), ALU.mult))
                yield
                last_step()
                rstep(V.tensor_tensor(sc[:, 0], sc[:, 0], K[:, 1:2].to_broadcast([P, CB, SW]), ALU.add))
                yield
                last_step()
                nodes = lambda ap: ap.rearrange("p s (t n) -> p s t n", t=T)
                spread_t = lambda ap: ap.unsqueeze(3).to_broadcast([P, CB, T, N])
                live = nodes(sc[:, 0, :, 0:TN])
                rstep(V.tensor_reduce(mx[:, 0], live, AX.X, ALU.max))
                yield
                last_step()
                V.tensor_tensor(nodes(sc[:, 1, :, 0:TN]), live, spread_t(mx[:, 0]), ALU.subtract).then_inc(shifted, 1)
                yield
                dve.wait_ge(exp_ready, i + 1)
                ex = nodes(sc[:, 2, :, 0:TN])
                rstep(V.tensor_reduce(mx[:, 1], ex, AX.X, ALU.add))
                yield
                last_step()
                rstep(V.reciprocal(mx[:, 2], mx[:, 1]))
                yield
                last_step()
                rstep(V.tensor_tensor(nodes(w[:, 2]), ex, spread_t(mx[:, 2]), ALU.mult))
                yield
                last_step()
                V.tensor_tensor(w[:, 0], w[:, 2], per_row(rs, TN), ALU.mult).then_inc(w_ready, 1)
                yield
                dve.wait_ge(w_ready, 2 * i + 1)
                V.tensor_tensor(w[:, 1], w[:, 0], per_row(nm, TN), ALU.mult).then_inc(w_ready, 1)

            def pool(i):
                next_steps = softmax(i + 1) if i + 1 < NBLK else iter(())
                dve.wait_ge(wT_ready, 3 * i + 1)
                V.tensor_tensor(w_lo[:], wT[:, 0], w_hi[:].bitcast(fp32), ALU.subtract).then_inc(w_lo_ready, 1)
                for k, c in enumerate(order):
                    g = i * FC + k
                    dve.wait_ge(wb_done, g + 1)
                    wait(dve, pr_used, g - 2)
                    V.scalar_tensor_tensor(out=pr[:, g % 3], in0=h[:, i % 2, c, :], scalar=nmu[:, c:c + 1], in1=wb_bank(g),
                                           op0=ALU.add, op1=ALU.mult).then_inc(pr_ready, 1)
                    if k == 3 and i:
                        result(i - 1)
                    if k >= POOL_FIRST:
                        for _ in range(2):
                            next(next_steps, None)
                dve.wait_ge(pr_used, FC * (i + 1))
                V.tensor_copy(O_sb[:], o_bank).then_inc(o_ready, 1)
                for _ in next_steps:
                    pass

            def result(i):
                dve.wait_ge(res_done, i + 1)
                if i >= 2:
                    dve.wait_ge(stored[i % 2], 16 * (i // 2))
                V.tensor_copy(res[:, i % 2], res_bank).then_inc(res_ready, 1)

            for _ in softmax(0):
                pass
            for i in range(NBLK):
                pool(i)
            result(NBLK - 1)

        @block.scalar
        def _(act):
            act.wait_ge(loaded, 16 * len(loads))
            nc.scalar.copy(spread[:].rearrange("p c f -> p (c f)"), spread_raw).then_inc(spread_ready, 1)
            act.wait_ge(step_done, ST_VARF)
            nc.scalar.activation(std[:], var[:], ACT.Sqrt, scale=1.0 / B, bias=eps[:]).then_inc(std_done, 1)
            act.wait_ge(step_done, ST_CSQ)

            def square(i, k):
                g, c = i * FC + k, order[k]
                act.wait_ge(h_loaded[i % 2][c % QC], 16 * CB * (i // 2 + 1))
                wait(act, sq_used, g - 3)
                nc.scalar.activation(sq[:, g % 4], h[:, i % 2, c, :], ACT.Square, bias=Csq[:, c:c + 1],
                                     scale=A[:, c:c + 1]).then_inc(sq_ready, 1)

            def copy_weights(i):
                for k in range(3):
                    act.wait_ge(wT_done, 3 * i + k + 1)
                    if k == 0:
                        wait(act, wb_done, FC * i)
                        wait(act, w_lo_ready, i)
                        wait(act, res_done, i)
                        nc.scalar.copy(w_hi[:], wT_bank(3 * i))
                    nc.scalar.copy(wT[:, k], wT_bank(3 * i + k)).then_inc(wT_ready, 1)

            for k in range(FC):
                square(0, k)
            for i in range(NBLK):
                first = ahead(i)
                act.wait_ge(var_ready, i + 1)
                nc.scalar.activation(st[:, 7], st[:, 6], ACT.Sqrt, bias=eps[:]).then_inc(rstd_ready, 1)
                for k in range(first // 2):
                    square(i + 1, k)
                act.wait_ge(shifted, i + 1)
                nc.scalar.activation(sc[:, 2, :, 0:TN], sc[:, 1, :, 0:TN], ACT.Exp).then_inc(exp_ready, 1)
                for k in range(first // 2, first):
                    square(i + 1, k)
                copy_weights(i)
                if i + 1 < NBLK:
                    for k in range(first, FC):
                        square(i + 1, k)

        @block.tensor
        def _(pe):
            MM = nc.tensor.matmul
            pe.wait_ge(fold_loaded, 16)
            pe.wait_ge(step_done, ST_MEAN)
            MM(k_bank[:, 0:TN], fold[:], fsum[:, 0], start=True, stop=True).then_inc(folded, 1)
            pe.wait_ge(step_done, ST_VAR)
            MM(k_bank[:, TN:2 * TN], fold[:], fsum[:, 1], start=True, stop=True).then_inc(folded, 1)
            pe.wait_ge(step_done, ST_VARF)

            def k_row(k, src):
                for q in range(FQ):
                    MM(k_bank[:, k * SW + q:k * SW + q + FQ * (FC - 1) + 1:FQ], quarter[:, q], src[:], start=True, stop=True)

            MM(k_bank[:, 3 * SW:3 * SW + 1], ones[:], sums[:, 0:1], start=True, stop=True).then_inc(k_done, 1)
            pe.wait_ge(step_done, ST_CSQ)
            k_row(0, LA)
            k_row(1, LBA)
            k_row(2, CLA)
            MM(k_bank[:, 3 * SW + 1:3 * SW + 2], ones[:], sums[:, 1:2], start=True, stop=True).then_inc(k_done, 1)
            pe.wait_ge(cols_ready, 1)

            def sums_of(i, k):
                g, c = i * FC + k, order[k]
                j = c // QC
                out_ = q_bank[D * j:D * j + D, :]
                if k == 0:
                    wait(pe, qs_ready, i)
                pe.wait_ge(h_loaded[i % 2][c % QC], 16 * CB * (i // 2 + 1))
                MM(out_, score_cols[:, c], h[:, i % 2, c, :], start=c % QC == 0, stop=False)
                pe.wait_ge(sq_ready, g + 1)
                last = MM(out_, square_mask[:], sq[:, g % 4], start=False, stop=c % QC == QC - 1 or c == FC - 1)
                last.then_inc(sq_used, 1)

            def turn_sums(i):
                pe.wait_ge(qs_ready, i + 1)
                wait(pe, qt_read, i)
                for s in range(CB):
                    last = nc.tensor.transpose(qt_bank[:, s * P:(s + 1) * P], qs[:, s * P:(s + 1) * P], ident[:])
                last.then_inc(qt_done, 1)

            def turn_weights(i, k):
                pe.wait_ge(w_ready, 2 * i + (1 if k == 0 else 2))
                wait(pe, wT_ready, 3 * i + k - 1)
                for s in range(CB):
                    last = nc.tensor.transpose(wT_bank(3 * i + k)[:, s * P:(s + 1) * P], w[:, k, s], ident[:])
                last.then_inc(wT_done, 1)

            def spread_weights(i, k):
                g, c = i * FC + k, order[k]
                wait(pe, pr_ready, g - 1)
                MM(wb_bank(g), spread[:, c], w_lo[:], start=True, stop=False)
                MM(wb_bank(g), spread[:, c], w_hi[:], start=False, stop=True).then_inc(wb_done, 1)

            def pool_chunk(i, k):
                g, c = i * FC + k, order[k]
                pe.wait_ge(pr_ready, g + 1)
                if k == 0:
                    wait(pe, o_ready, i)
                parts = [(0, c), (1, FC)] if c == half else [(int(c > half), c)]
                for t, col in parts:
                    j = 2 * t + c % 2
                    in_group = [x for x in order if x % 2 == c % 2 and (x <= half if t == 0 else x >= half)]
                    last = MM(o_bank[D * j:D * j + D, :], pool_cols[:, col], pr[:, g % 3],
                              start=c == in_group[0], stop=c == in_group[-1])
                last.then_inc(pr_used, 1)

            def finish(i):
                last = None
                pe.wait_ge(o_ready, i + 1)
                pe.wait_ge(wT_ready, 3 * i + 3)
                wait(pe, res_ready, i)
                MM(res_bank, fold_out[:], O_sb[:], start=True, stop=False)
                for k in range(3):
                    last = MM(res_bank, rowblk[:, k].rearrange("p t d -> p (t d)"), wT[:, k], start=False, stop=k == 2)
                last.then_inc(res_done, 1)

            for k in range(FC):
                sums_of(0, k)
            turn_sums(0)
            for i in range(NBLK):
                left = list(range(FC)) if i + 1 < NBLK else []
                while left and left[0] < ahead(i):
                    sums_of(i + 1, left.pop(0))
                if i == 0:
                    pe.wait_ge(cols_ready, 2)
                turn_weights(i, 0)
                pe.wait_ge(w_lo_ready, i + 1)
                for k in range(FC):
                    spread_weights(i, k)
                    if k == 0:
                        turn_weights(i, 1)
                        turn_weights(i, 2)
                    for _ in range(2):
                        if left:
                            sums_of(i + 1, left.pop(0))
                    if k >= 2:
                        pool_chunk(i, k - 2)
                    if k == POOL_FIRST and i + 1 < NBLK:
                        assert not left
                        turn_sums(i + 1)
                pool_chunk(i, FC - 2)
                pool_chunk(i, FC - 1)
                finish(i)


ST_MEAN = 5
ST_VAR = ST_MEAN + 5
ST_LA = ST_VAR + 3
ST_VARF = ST_LA + 2 * FQ
ST_CSQ = ST_VARF + 9


def program(nc, ins, out):
    adjT = nc.dram_tensor("adjT", [TILES, N, TN, P], fp32, kind="Internal").ap()
    hF = nc.dram_tensor("hF", [TILES, P, FC, P], fp32, kind="Internal").ap()
    with nc.psum_tensor("psum", [P, 8 * BANK], fp32) as psum:
        stage1(nc, psum, ins["xT"], ins["W"], adjT, ins["ident"])
        with nc.sbuf_tensor("means", [P, TILES, TN], fp32) as means, nc.sbuf_tensor("devs", [P, TILES, TN], fp32) as devs:
            stage2(nc, psum, ins, adjT, hF, (means, devs))
            stage3(nc, psum, ins, hF, (means, devs), out)


def masks(np, dtype):
    q, d = np.divmod(np.arange(P), D)
    c, r, tn = np.arange(FC), np.arange(D), np.arange(TN)
    masker = (FQ * c[None, :] + q[:, None]) // N
    pool = (d[:, None, None] == r) & np.ones((P, FC + 1, 1), bool)
    mixed = FC // 2
    pool[:, mixed] &= (masker[:, mixed] == 0)[:, None]
    pool[:, FC] &= (masker[:, mixed] == 1)[:, None]
    found = {
        "score_mask": r == FQ * (c % QC)[None, :, None] + q[:, None, None],
        "square_mask": (r == QR + 1) & np.ones((P, 1), bool),
        "pool_mask": pool,
        "quarter": (q[:, None, None] == np.arange(FQ)[:, None]) & np.ones((1, 1, P), bool),
        "spread": (tn[:, None, None] == FQ * c[:, None] + q).reshape(TN, FC * P),
        "fold_out": (q[:, None] // 2 == np.arange(T * D) // D) & (d[:, None] == np.arange(T * D) % D),
        "t_mask": tn[:, None] // N == np.arange(T),
    }
    return {name: a.astype(dtype) for name, a in found.items()}


def kernel(r_x, L0_rec_masker_param, L0_rec_masker_bias, L0_rec_weight, L0_rec_w_ih, L0_rec_w_hh, L0_rec_b_ih, L0_rec_b_hh,
           L0_rec_bn_gamma, L0_rec_bn_beta, L0_rec_ln_gamma, L0_rec_ln_beta, L0_rec_attn_w, L0_rec_attn_b):
    import numpy as np
    import concourse.bacc as bacc
    from concourse.bass_utils import run_bass_kernel_spmd

    x = np.asarray(r_x)
    to = lambda a: np.asarray(a)
    gates = np.stack([to(L0_rec_b_ih).reshape(3, D), to(L0_rec_b_hh).reshape(3, D)]).transpose(2, 0, 1)

    def chunks(a, below):
        rest, zeros = a[KF * P:], np.zeros((BIAS_HI - KR - 1, a.shape[1]), a.dtype)
        return np.concatenate([a[:KF * P], rest, rest, rest, below, zeros, below])

    arrays = {
        "xT": chunks(x.reshape(B, KX).T, np.ones((1, B), x.dtype)),
        "W": chunks(to(L0_rec_masker_param).transpose(1, 0, 2).reshape(KX, T * N * N),
                    to(L0_rec_masker_bias).reshape(1, T * N * N)),
        "ident": np.eye(P, dtype=x.dtype),
        "fold": np.tile(np.eye(D, dtype=x.dtype), (4, 4)),
        "xm": x.transpose(1, 0, 2),
        "xg": x.reshape(TILES, 4, 32, N, D).transpose(0, 1, 4, 2, 3).reshape(TILES, P, 32, N),
        "wT4": np.tile(to(L0_rec_weight)[0].T, (1, 4)),
        "wihT": to(L0_rec_w_ih).T,
        "whhT4": np.tile(to(L0_rec_w_hh).T, (4, 1)),
        "biases": np.tile(gates, (4, 1, 1)),
        "par": np.stack([to(a).reshape(FC, FQ, D).transpose(1, 2, 0).reshape(P, FC)
                         for a in (L0_rec_bn_gamma, L0_rec_bn_beta, L0_rec_ln_gamma, L0_rec_ln_beta)], axis=1),
        "rowpar": np.stack([to(a).reshape(TN, D) for a in (L0_rec_bn_beta, L0_rec_ln_gamma, L0_rec_ln_beta)], axis=1),
        "aw": np.tile(to(L0_rec_attn_w).reshape(D, 1), (FQ, 1)),
        "attn_b": to(L0_rec_attn_b).reshape(1),
        **masks(np, x.dtype),
    }
    arrays = {name: np.ascontiguousarray(a) for name, a in arrays.items()}
    nc = bacc.Bacc("TRN2", target_bir_lowering=False, num_devices=1)
    ins = {name: nc.dram_tensor(name, a.shape, mybir.dt.from_np(a.dtype), kind="ExternalInput").ap() for name, a in arrays.items()}
    out = nc.dram_tensor("out", [T * D, B], fp32, kind="ExternalOutput").ap()
    program(nc, ins, out)
    result = run_bass_kernel_spmd(nc, [arrays], core_ids=[0])
    return np.ascontiguousarray(result.results[0]["out"].T)
```
